# Optimizing a Trainium2 kernel written in Bass

```python
import numpy as np
import jax
import jax.numpy as jnp

def _softmax(x, axis=-1):
    return jax.nn.softmax(x, axis=axis)

def _gelu(x):
    return jax.nn.gelu(x, approximate=True)

def _silu(x):
    return jax.nn.silu(x)

def _sigmoid(x):
    return jax.nn.sigmoid(x)

def _layernorm(x, axis=-1, eps=1e-05):
    m = jnp.mean(x, axis=axis, keepdims=True)
    v = jnp.var(x, axis=axis, keepdims=True)
    return (x - m) / jnp.sqrt(v + eps)

def _scatter_add(tgt, idx, src, axis=0):
    return tgt.at[idx].add(src)

def _segment_sum(src, seg, n):
    return jax.ops.segment_sum(src, seg, n)
kernel_name = 'mk_conv_seq_d4_conv_nhwc768_r2_fec910'

def setup_inputs(seed: int=0):
    np.random.seed(seed)
    _w = jnp.asarray

    def _rec_inputs():
        import jax
        import jax.numpy as jnp
        _gk = jax.random.key(seed)
        x = -4.65e-05 + 0.9999 * jax.random.normal(jax.random.fold_in(_gk, 1), (2, 64, 64, 384), jnp.float32)
        return x
    x = _rec_inputs()

    def _L0_conv_setup():
        import jax, jax.numpy as jnp
        import numpy as np
        NUM_HEADS = 8
        HIDDEN_SIZE = 384
        BLOCK = HIDDEN_SIZE // NUM_HEADS
        FACTOR = 1
        LAMBDA = 0.01
        FRACTION = 1.0
        SCALE = 0.02

        def softshrink(x, lambd):
            return jnp.where(x > lambd, x - lambd, jnp.where(x < -lambd, x + lambd, jnp.zeros_like(x)))
        key = jax.random.key(seed)
        k = jax.random.split(key, 5)
        B, H, W = (4, 64, 64)
        x = jax.random.normal(k[0], (B, H, W, HIDDEN_SIZE), dtype=jnp.float32)
        w1 = SCALE * jax.random.normal(k[1], (2, NUM_HEADS, BLOCK, BLOCK * FACTOR), dtype=jnp.float32)
        b1 = SCALE * jax.random.normal(k[2], (2, NUM_HEADS, BLOCK * FACTOR), dtype=jnp.float32)
        w2 = SCALE * jax.random.normal(k[3], (2, NUM_HEADS, BLOCK * FACTOR, BLOCK), dtype=jnp.float32)
        b2 = SCALE * jax.random.normal(k[4], (2, NUM_HEADS, BLOCK), dtype=jnp.float32)
        return {'x': x, 'w1': w1, 'b1': b1, 'w2': w2, 'b2': b2}
    _L0_conv_all = _L0_conv_setup()
    _L0_conv_in = {k: v for k, v in _L0_conv_all.items() if k in ('w1', 'b1', 'w2', 'b2')}
    del _L0_conv_all

    def _L1_conv_setup():
        import jax, jax.numpy as jnp
        import numpy as np

        def _dht(x):
            f = jnp.fft.fftn(x)
            return f.real + f.imag
        key = jax.random.key(seed)
        ks = jax.random.split(key, 5)
        B, H, W, C = (2, 64, 128, 384)
        nb, fac = (8, 1)
        bs = C // nb
        scale = 0.02
        x = jax.random.normal(ks[0], (B, H, W, C), dtype=jnp.float32)
        w1 = scale * jax.random.normal(ks[1], (2, nb, bs, bs * fac), dtype=jnp.float32)
        b1 = scale * jax.random.normal(ks[2], (2, nb, bs * fac), dtype=jnp.float32)
        w2 = scale * jax.random.normal(ks[3], (2, nb, bs * fac, bs), dtype=jnp.float32)
        b2 = scale * jax.random.normal(ks[4], (2, nb, bs), dtype=jnp.float32)
        return {'x': x, 'w1': w1, 'b1': b1, 'w2': w2, 'b2': b2}
    _L1_conv_all = _L1_conv_setup()
    _L1_conv_in = {k: v for k, v in _L1_conv_all.items() if k in ('w1', 'b1', 'w2', 'b2')}
    del _L1_conv_all

    def _L2_conv_setup():
        import jax, jax.numpy as jnp
        import numpy as np
        SPARSITY_THRESHOLD = 0.01
        HARD_THRESH_FRAC = 1.0

        def softshrink(x, lam):
            return jnp.where(x > lam, x - lam, jnp.where(x < -lam, x + lam, jnp.zeros_like(x)))

        def compl_mul_add_act(a, b, c):
            tmp = jnp.einsum('bxykis,kiot->stbxyko', a, b)
            real = tmp[0, 0] - tmp[1, 1]
            imag = tmp[1, 0] + tmp[0, 1]
            return jnp.stack([real, imag], axis=-1) + c
        key = jax.random.key(seed)
        k = jax.random.split(key, 5)
        B, H, W, C = (1, 128, 128, 384)
        nb, bs, factor = (8, 48, 1)
        scale = 0.02
        return {'x': jax.random.normal(k[0], (B, H, W, C), dtype=jnp.float32), 'w1': scale * jax.random.normal(k[1], (nb, bs, bs * factor, 2), dtype=jnp.float32), 'b1': scale * jax.random.normal(k[2], (nb, bs * factor, 2), dtype=jnp.float32), 'w2': scale * jax.random.normal(k[3], (nb, bs * factor, bs, 2), dtype=jnp.float32), 'b2': scale * jax.random.normal(k[4], (nb, bs, 2), dtype=jnp.float32)}
    _L2_conv_all = _L2_conv_setup()
    _L2_conv_in = {k: v for k, v in _L2_conv_all.items() if k in ('w1', 'b1', 'w2', 'b2')}
    del _L2_conv_all

    def _L3_conv_setup():
        import jax, jax.numpy as jnp
        import numpy as np
        HIDDEN = 384
        NUM_BLOCKS = 8
        BLOCK = HIDDEN // NUM_BLOCKS
        FACTOR = 1
        LAMBDA = 0.01
        SCALE = 0.02

        def _softshrink(v, lam):
            return jnp.sign(v) * jnp.maximum(jnp.abs(v) - lam, 0.0)
        key = jax.random.key(seed)
        k0, k1, k2, k3, k4 = jax.random.split(key, 5)
        B, H, W, C = (4, 64, 64, HIDDEN)
        x = jax.random.normal(k0, (B, H, W, C), dtype=jnp.float32)
        w1 = SCALE * jax.random.normal(k1, (2, NUM_BLOCKS, BLOCK, BLOCK * FACTOR), dtype=jnp.float32)
        b1 = SCALE * jax.random.normal(k2, (2, NUM_BLOCKS, BLOCK * FACTOR), dtype=jnp.float32)
        w2 = SCALE * jax.random.normal(k3, (2, NUM_BLOCKS, BLOCK * FACTOR, BLOCK), dtype=jnp.float32)
        b2 = SCALE * jax.random.normal(k4, (2, NUM_BLOCKS, BLOCK), dtype=jnp.float32)
        return {'x': x, 'w1': w1, 'b1': b1, 'w2': w2, 'b2': b2}
    _L3_conv_all = _L3_conv_setup()
    _L3_conv_in = {k: v for k, v in _L3_conv_all.items() if k in ('w1', 'b1', 'w2', 'b2')}
    del _L3_conv_all
    return {'x': x, 'L0_conv_w1': _L0_conv_in['w1'], 'L0_conv_b1': _L0_conv_in['b1'], 'L0_conv_w2': _L0_conv_in['w2'], 'L0_conv_b2': _L0_conv_in['b2'], 'L1_conv_w1': _L1_conv_in['w1'], 'L1_conv_b1': _L1_conv_in['b1'], 'L1_conv_w2': _L1_conv_in['w2'], 'L1_conv_b2': _L1_conv_in['b2'], 'L2_conv_w1': _L2_conv_in['w1'], 'L2_conv_b1': _L2_conv_in['b1'], 'L2_conv_w2': _L2_conv_in['w2'], 'L2_conv_b2': _L2_conv_in['b2'], 'L3_conv_w1': _L3_conv_in['w1'], 'L3_conv_b1': _L3_conv_in['b1'], 'L3_conv_w2': _L3_conv_in['w2'], 'L3_conv_b2': _L3_conv_in['b2']}

def reference(x, L0_conv_w1, L0_conv_b1, L0_conv_w2, L0_conv_b2, L1_conv_w1, L1_conv_b1, L1_conv_w2, L1_conv_b2, L2_conv_w1, L2_conv_b1, L2_conv_w2, L2_conv_b2, L3_conv_w1, L3_conv_b1, L3_conv_w2, L3_conv_b2):
    import jax
    import jax.numpy as jnp

    def _L0_conv_ref(x, w1, b1, w2, b2):
        import jax, jax.numpy as jnp
        import numpy as np
        NUM_HEADS = 8
        HIDDEN_SIZE = 384
        BLOCK = HIDDEN_SIZE // NUM_HEADS
        FACTOR = 1
        LAMBDA = 0.01
        FRACTION = 1.0
        SCALE = 0.02

        def softshrink(x, lambd):
            return jnp.where(x > lambd, x - lambd, jnp.where(x < -lambd, x + lambd, jnp.zeros_like(x)))
        bias = x
        dtype = x.dtype
        xf32 = x.astype(jnp.float32)
        B, H, W, C = x.shape
        xs = jnp.fft.rfft2(xf32, axes=(1, 2))
        Wm = W // 2 + 1
        xs = xs.reshape(B, H, Wm, NUM_HEADS, BLOCK)
        total_modes = H // 2 + 1
        kept = int(total_modes * FRACTION)
        lo, hi = (total_modes - kept, min(total_modes + kept, H))
        wk = min(kept, Wm)
        xr = jnp.real(xs[:, lo:hi, :wk])
        xi = jnp.imag(xs[:, lo:hi, :wk])
        o1r = jax.nn.relu(jnp.einsum('bxyhi,hio->bxyho', xr, w1[0]) - jnp.einsum('bxyhi,hio->bxyho', xi, w1[1]) + b1[0])
        o1i = jax.nn.relu(jnp.einsum('bxyhi,hio->bxyho', xi, w1[0]) + jnp.einsum('bxyhi,hio->bxyho', xr, w1[1]) + b1[1])
        o2r = jnp.einsum('bxyho,hoi->bxyhi', o1r, w2[0]) - jnp.einsum('bxyho,hoi->bxyhi', o1i, w2[1]) + b2[0]
        o2i = jnp.einsum('bxyho,hoi->bxyhi', o1i, w2[0]) + jnp.einsum('bxyho,hoi->bxyhi', o1r, w2[1]) + b2[1]
        zr = jnp.zeros((B, H, Wm, NUM_HEADS, BLOCK), dtype=jnp.float32).at[:, lo:hi, :wk].set(o2r)
        zi = jnp.zeros((B, H, Wm, NUM_HEADS, BLOCK), dtype=jnp.float32).at[:, lo:hi, :wk].set(o2i)
        out_c = softshrink(zr, LAMBDA) + 1j * softshrink(zi, LAMBDA)
        out_c = out_c.reshape(B, H, Wm, C)
        out = jnp.fft.irfft2(out_c, s=(H, W), axes=(1, 2))
        return out.astype(dtype) + bias

    def _L1_conv_ref(x, w1, b1, w2, b2):
        import jax, jax.numpy as jnp
        import numpy as np

        def _dht(x):
            f = jnp.fft.fftn(x)
            return f.real + f.imag
        SPARSITY = 0.01
        FRAC = 1.0
        bias = x
        B, H, W, C = x.shape
        nb = w1.shape[1]
        bs = C // nb
        xf = x.astype(jnp.float32)
        X_k = _dht(xf).reshape(B, H, W, nb, bs)
        X_nk = jnp.roll(jnp.flip(xf, axis=(1, 2)), shift=(1, 1), axis=(1, 2)).reshape(B, H, W, nb, bs)
        total = H // 2 + 1
        kept = int(total * FRAC)
        r0, r1 = (total - kept, min(total + kept, H))
        a = X_k[:, r0:r1, :kept]
        an = X_nk[:, r0:r1, :kept]
        ein = lambda t, w: jnp.einsum('bhwni,nio->bhwno', t, w)
        o1_k = jax.nn.relu(0.5 * (ein(a, w1[0]) - ein(an, w1[1]) + ein(a, w1[1]) + ein(an, w1[0])) + b1[0])
        o1_nk = jax.nn.relu(0.5 * (ein(an, w1[0]) - ein(a, w1[1]) + ein(an, w1[1]) + ein(a, w1[0])) + b1[1])
        o2_k = 0.5 * (ein(o1_k, w2[0]) - ein(o1_nk, w2[1]) + ein(o1_k, w2[1]) + ein(o1_nk, w2[0])) + b2[0]
        o2_nk = 0.5 * (ein(o1_nk, w2[0]) - ein(o2_k, w2[1]) + ein(o1_nk, w2[1]) + ein(o2_k, w2[0])) + b2[1]
        s = o2_k + o2_nk
        s = jnp.sign(s) * jnp.maximum(jnp.abs(s) - SPARSITY, 0.0)
        full = jnp.zeros((B, H, W, nb, bs), jnp.float32).at[:, r0:r1, :kept].set(s)
        full = full.reshape(B, H, W, C)
        out = _dht(full) / full.size
        return out.astype(x.dtype) + bias

    def _L2_conv_ref(x, w1, b1, w2, b2):
        import jax, jax.numpy as jnp
        import numpy as np
        SPARSITY_THRESHOLD = 0.01
        HARD_THRESH_FRAC = 1.0

        def softshrink(x, lam):
            return jnp.where(x > lam, x - lam, jnp.where(x < -lam, x + lam, jnp.zeros_like(x)))

        def compl_mul_add_act(a, b, c):
            tmp = jnp.einsum('bxykis,kiot->stbxyko', a, b)
            real = tmp[0, 0] - tmp[1, 1]
            imag = tmp[1, 0] + tmp[0, 1]
            return jnp.stack([real, imag], axis=-1) + c
        bias = x
        dtype = x.dtype
        B, H, W, C = x.shape
        nb, bs = (w1.shape[0], w1.shape[1])
        total_modes = H // 2 + 1
        kept_modes = int(total_modes * HARD_THRESH_FRAC)
        lo = total_modes - kept_modes
        hi = min(total_modes + kept_modes, H)
        xf = jnp.fft.rfft2(x.astype(jnp.float32), axes=(1, 2), norm='ortho')
        xf = xf.reshape(B, H, W // 2 + 1, nb, bs)
        xs = jnp.stack([xf.real, xf.imag], axis=-1)
        sub = xs[:, lo:hi, :kept_modes]
        o1 = jax.nn.relu(compl_mul_add_act(sub, w1, b1))
        o2 = jnp.zeros_like(xs).at[:, lo:hi, :kept_modes].set(compl_mul_add_act(o1, w2, b2))
        o2 = softshrink(o2, SPARSITY_THRESHOLD)
        xc = (o2[..., 0] + 1j * o2[..., 1]).reshape(B, H, W // 2 + 1, C)
        out = jnp.fft.irfft2(xc, s=(H, W), axes=(1, 2), norm='ortho').astype(dtype)
        return out + bias

    def _L3_conv_ref(x, w1, b1, w2, b2):
        import jax, jax.numpy as jnp
        import numpy as np
        HIDDEN = 384
        NUM_BLOCKS = 8
        BLOCK = HIDDEN // NUM_BLOCKS
        FACTOR = 1
        LAMBDA = 0.01
        SCALE = 0.02

        def _softshrink(v, lam):
            return jnp.sign(v) * jnp.maximum(jnp.abs(v) - lam, 0.0)
        bias = x
        dtype = x.dtype
        B, H, W, C = x.shape
        xf = jnp.fft.rfft2(x.astype(jnp.float32), axes=(1, 2), norm='ortho')
        xf = xf.reshape(B, H, W // 2 + 1, NUM_BLOCKS, BLOCK)
        xr, xi = (xf.real, xf.imag)
        o1r = jax.nn.relu(jnp.einsum('bhwni,nio->bhwno', xr, w1[0]) - jnp.einsum('bhwni,nio->bhwno', xi, w1[1]) + b1[0])
        o1i = jax.nn.relu(jnp.einsum('bhwni,nio->bhwno', xi, w1[0]) + jnp.einsum('bhwni,nio->bhwno', xr, w1[1]) + b1[1])
        o2r = jnp.einsum('bhwni,nio->bhwno', o1r, w2[0]) - jnp.einsum('bhwni,nio->bhwno', o1i, w2[1]) + b2[0]
        o2i = jnp.einsum('bhwni,nio->bhwno', o1i, w2[0]) + jnp.einsum('bhwni,nio->bhwno', o1r, w2[1]) + b2[1]
        o = jnp.stack([o2r, o2i], axis=-1)
        o = _softshrink(o, LAMBDA)
        xc = jax.lax.complex(o[..., 0], o[..., 1]).reshape(B, H, W // 2 + 1, C)
        out = jnp.fft.irfft2(xc, s=(H, W), axes=(1, 2), norm='ortho')
        return out.astype(dtype) + bias

    def _gn(v, G=32, eps=1e-05):
        B_, H_, W_, C_ = v.shape
        g = v.reshape(B_, H_, W_, G, C_ // G)
        m = jnp.mean(g, axis=(1, 2, 4), keepdims=True)
        s = jnp.var(g, axis=(1, 2, 4), keepdims=True)
        return ((g - m) / jnp.sqrt(s + eps)).reshape(v.shape)

    def _ln_c(v, eps=1e-06):
        m = jnp.mean(v, axis=-1, keepdims=True)
        s = jnp.var(v, axis=-1, keepdims=True)
        return (v - m) / jnp.sqrt(s + eps)

    def _ln_t(v, eps=1e-05):
        m = jnp.mean(v, axis=-1, keepdims=True)
        s = jnp.var(v, axis=-1, keepdims=True)
        return (v - m) / jnp.sqrt(s + eps)

    def _to_tokens(v):
        B_, H_, W_, C_ = v.shape
        return v.reshape(B_, H_ * W_, C_)

    def _from_tokens(t, like):
        return t.reshape(like.shape)
    x = _L0_conv_ref(x, L0_conv_w1, L0_conv_b1, L0_conv_w2, L0_conv_b2)
    x = _L1_conv_ref(x, L1_conv_w1, L1_conv_b1, L1_conv_w2, L1_conv_b2)
    x = _L2_conv_ref(x, L2_conv_w1, L2_conv_b1, L2_conv_w2, L2_conv_b2)
    x = _L3_conv_ref(x, L3_conv_w1, L3_conv_b1, L3_conv_w2, L3_conv_b2)
    return x

_drawn_inputs = setup_inputs


def setup_inputs(seed=0):
    import zlib

    import numpy as np

    out = dict(_drawn_inputs(seed))
    spreads = {}
    factors = {'L0_conv_b1': 64.0,
     'L0_conv_b2': 64.0,
     'L1_conv_w1': 8.0,
     'L1_conv_b1': 64.0,
     'L1_conv_w2': 5.922,
     'L1_conv_b2': 64.0,
     'L2_conv_w1': 3.355,
     'L2_conv_b1': 8.0,
     'L2_conv_w2': 2.771,
     'L3_conv_w1': 3.292,
     'L3_conv_b1': 8.0,
     'L3_conv_w2': 2.727}
    for name, (base, spread) in spreads.items():
        noise = np.random.default_rng([zlib.crc32(name.encode()), seed]).standard_normal(out[name].shape)
        drawn = base * np.exp(spread * noise) if base else spread * noise
        out[name] = jnp.asarray(drawn.astype(out[name].dtype))
    for name, factor in factors.items():
        out[name] = (out[name] * factor).astype(out[name].dtype)
    return out
```

```python
import numpy as np

B, H, W, C = 2, 64, 64, 384
NB = 8
BS = C // NB
P = 128
NT = C // P
HP = H // 2
KW = W // 2 + 1
Q = 64
TOK = H * W
BANK = 512
BANKS = 8
ONE = BS
HALF = 64
MROWS = HALF + BS
LAMBDA = 0.01

S1_GROUP = 3
S1_UNITS = -(-HP // S1_GROUP)
T_GROUP = BANK // P
T1_UNITS = -(-KW // T_GROUP)
M_GROUP = BANK // H
M_GROUPS = -(-KW // M_GROUP)
STEPS = NB * M_GROUPS
INV_UNITS = Q * H // BANK
PAIRS = -(-KW // 2)
PREP_OPERANDS, PREP_STEPS = 10, 15
TAIL = 5 * INV_UNITS


def group(n, size, total):
    return n * size, min(size, total - n * size)


def forward_order():
    s1 = [[("S1", t, g) for g in range(S1_UNITS)] for t in range(NT)]
    t1 = [[("T1", t, g) for g in range(T1_UNITS)] for t in range(NT)]
    return s1[0] + s1[1] + t1[0] + s1[2] + t1[1] + t1[2]


def inverse_order():
    s5, t2, s6 = ([[(s, t, u) for u in range(INV_UNITS)] for t in range(NT)] for s in ("S5", "T2", "S6"))
    return s5[0] + s5[1] + t2[0] + s5[2] + t2[1] + s6[0] + t2[2] + s6[1] + s6[2]


def conv_order():
    mid = []
    for n in range(STEPS + 2):
        mid += [(s, n - lag) for lag, s in enumerate(("S2", "S3", "S4")) if 0 <= n - lag < STEPS]
    return forward_order() + mid + inverse_order()


def hartley_order():
    def cols(m):
        return range(group(m, 2, KW)[1])
    mid = [("F2", 0, k) for k in cols(0)] + [("CF", 0)]
    for m in range(PAIRS):
        mid += [("TJ", m, 0), ("TJ", m, 1)]
        if m + 1 < PAIRS:
            mid += [("F2", m + 1, k) for k in cols(m + 1)]
        mid += [("H1", m, 0), ("H1", m, 1)]
        if m + 1 < PAIRS:
            mid += [("CF", m + 1)]
        mid += [("H2", m)]
        if m > 0:
            mid += [("CI", m - 1, k) for k in cols(m - 1)]
    mid += [("CI", PAIRS - 1, k) for k in cols(PAIRS - 1)]
    return forward_order() + mid + inverse_order()


class Counts:

    VECTOR = {"S4", "S6", "CF", "H2", "CI"}
    SCALAR = {"S2", "S3", "F2", "TJ", "H1"}

    def __init__(self, order):
        self.order = order
        self.unit, self.by, self.emptied = {}, {}, {}
        self.vec = self.act = 0
        for n, key in enumerate(order):
            self.unit[key] = n
            self.by[key] = ("vec" if key[0] in self.VECTOR else "act" if key[0] in self.SCALAR
                            else ("vec", "act")[key[2] % 2])
            if self.by[key] == "vec":
                self.vec += 1
                self.emptied[key] = self.vec
            else:
                self.act += 1
                self.emptied[key] = self.act
        self.fills = len(order)


def constants():
    def cos(a, n):
        return np.cos(2 * np.pi * (a % n) / n).round(17) + 0.0

    def sin(a, n):
        a = a % n
        s = np.sin(2 * np.pi * a / n)
        return np.where((2 * a) % n == 0, 0.0, s)

    k64, h64 = np.arange(64), np.arange(64)
    kw = np.arange(KW)
    cw, sw = cos(np.outer(h64, kw), 64), sin(np.outer(h64, kw), 64)
    dft_w = np.zeros((2, W, 2, 2, KW))
    for j in range(2):
        dft_w[j, :, 0, j] = cw
        dft_w[j, :, 1, j] = -sw
    rows = np.array([2 * hp + j for j in range(2) for hp in range(HP)])
    ch, sh = cos(np.outer(rows, k64), 64), sin(np.outer(rows, k64), 64)
    re, im = np.concatenate([ch, sh]), np.concatenate([-sh, ch])
    dft_h = np.concatenate([re, im], 1)
    flip = -k64 % 64
    dft_h_uv = np.concatenate([(re + im)[:, flip], (im - re)[:, flip]], 1)
    ch, sh = ch.T, sh.T
    zr, zi = np.concatenate([ch, -sh]), np.concatenate([sh, ch])
    inv_h = np.concatenate([zr, zi, zr], 1)
    ch, sh = ch[flip], sh[flip]
    zr, zi = np.concatenate([ch, sh]), np.concatenate([-sh, ch])
    inv_h_dht = np.concatenate([zr, zi, zr + zi], 1)
    inv_w, inv_w_dht = np.zeros((2, 2, Q, 2, W))
    cw, sw = cw.T, sw.T
    for j in range(2):
        for q, k in ((0, 0), (1, 32)):
            inv_w[j, q, j] = cw[k]
            inv_w_dht[j, q, j] = cw[k]
        for k in range(1, 32):
            inv_w[j, 2 * k, j] = 2 * cw[k]
            inv_w[j, 2 * k + 1, j] = -2 * sw[k]
            inv_w_dht[j, 2 * k, j] = cw[k] - sw[k]
            inv_w_dht[j, 2 * k + 1, j] = cw[k] + sw[k]
    cc = np.outer(np.arange(C), np.arange(C))
    ccos, csin = cos(cc, C), sin(cc, C)
    fwd_c = np.stack([ccos.reshape(NT, P, C), csin.reshape(NT, P, C)], 1)
    fwd_c = fwd_c.transpose(2, 0, 1, 3)
    inv_c = np.zeros((2, HALF, NB // 2, 2, C))
    for b in range(NB):
        inv_c[b % 2, :BS, b // 2, 0] = ccos[b * BS:(b + 1) * BS]
        inv_c[b % 2, :BS, b // 2, 1] = -csin[b * BS:(b + 1) * BS]
    sign = np.ones((P, 2))
    sign[:, 1] = -1
    parts = {"identity": np.eye(P), "dft_w": dft_w, "dft_h": dft_h, "dft_h_uv": dft_h_uv, "inv_h": inv_h,
             "inv_h_dht": inv_h_dht, "inv_w": inv_w, "inv_w_dht": inv_w_dht, "sign": sign}
    parts = {n: a.reshape(P, -1).astype(np.float32) for n, a in parts.items()}
    return parts, fwd_c.reshape(P, -1).astype(np.float32), inv_c.reshape(P, -1).astype(np.float32)


def block_rows(b):
    first = min(b * BS, C - HALF)
    return first, b * BS - first


def build(nc, x, consts, fwd_c_dram, inv_c_dram, conv_w3, conv_w4, conv_bias, l1_w3, l1_w3_bias, l1_q, l1_e, l1_t,
          out, const_at):
    import concourse.bass as bass
    from concourse import mybir
    from contextlib import ExitStack

    F32 = mybir.dt.float32
    ALU = mybir.AluOpType
    ACT = mybir.ActivationFunctionType
    conv, dht = Counts(conv_order()), Counts(hartley_order())

    ctx = ExitStack()
    with ctx:
        def sb(name, shape):
            return ctx.enter_context(nc.sbuf_tensor(name, shape, F32))

        def sem(name):
            return ctx.enter_context(nc.semaphore(name))

        def dram(name, shape):
            return nc.dram_tensor(name, shape, F32, kind="Internal").ap()

        after_l0 = dram("after_l0", (B, TOK, C))
        after_l1 = dram("after_l1", (B, TOK, C))
        l1_first = dram("l1_first", (MROWS, NB * MROWS))
        l1_second = dram("l1_second", (MROWS, NB * HALF))

        X = sb("X", [P, NT, HP, P])
        Bm = sb("Bm", [P, KW, C])
        D = sb("D", [P, KW, C])
        ring = sb("ring", [P, 2 * P * KW])
        const = sb("const", [P, consts.shape[1]])
        tables = sb("tables", [P, (2 * NT + NB) * C])

        warm = sb("warm", [P, 2])

        def cst(name):
            at, n = const_at[name]
            return const[:, at:at + n]

        identity, dft_w, dft_h, dft_h_uv = (cst(n) for n in ("identity", "dft_w", "dft_h", "dft_h_uv"))
        sign = cst("sign")

        def A(t):
            return ring[:, (t % 2) * P * KW:(t % 2 + 1) * P * KW].rearrange("p (r k) -> p r k", k=KW)

        def E(t):
            at = (t % 2) * P * HP
            return ring[:, at:at + P * HP].rearrange("p (r h) -> p r h", h=HP)

        def G(t):
            return Bm[:, :, :].rearrange("p k c -> p (k c)")[:, (t % 2) * HP * P:(t % 2 + 1) * HP * P]

        def in_ring(sizes):
            at, views = 0, []
            for n in sizes:
                views.append(ring[:, at:at + n])
                at += n
            assert at <= 2 * P * KW
            return views

        modes0, modes1, hidden0, hidden1, clip0, clip1 = in_ring([BANK] * 6)
        modes, hidden, clip = (modes0, modes1), (hidden0, hidden1), (clip0, clip1)
        UV, J0, J1, pair0, pair1, hid0, hid1, shrunk0, shrunk1, clip_l1, w3_l1, w4_l1 = in_ring(
            [2 * NT * P, NB * MROWS, NB * MROWS] + [BANK] * 7 + [NB * MROWS, NB * HALF])
        UV = UV.rearrange("p (a n) -> p a n", n=P)
        J = [v.rearrange("p (b r) -> p b r", r=MROWS) for v in (J0, J1)]
        pair, hid, shrunk = (pair0, pair1), (hid0, hid1), (shrunk0, shrunk1)
        w3_l1 = w3_l1.rearrange("p (b r) -> p b r", r=MROWS)
        w4_l1 = w4_l1.rearrange("p (b r) -> p b r", r=HALF)

        fwd_c = tables[:, 0:2 * NT * C].rearrange("p (a c) -> p a c", c=C)
        inv_c = tables[:, 2 * NT * C:].rearrange("p (g a c) -> p g a c", a=2, c=C)
        W3, W4 = NB * MROWS, NB * 2 * BS
        slot = W3 + W4 + NB

        def weights(layer):
            at = (layer == 3) * slot
            return (tables[:, at:at + W3].rearrange("p (b r) -> p b r", r=MROWS),
                    tables[:, at + W3:at + W3 + W4].rearrange("p (b r) -> p b r", r=2 * BS),
                    tables[:, at + W3 + W4:at + slot])

        Dflat = D[:, :, :].rearrange("p k c -> p (k c)")
        prep, at = {}, 0
        for name, n in (("v0", NB * MROWS), ("v1", NB * MROWS), ("v", NB * MROWS), ("q0", NB * MROWS), ("q1", NB * MROWS),
                        ("q", NB * MROWS), ("e0", NB * BS), ("e1", NB * BS), ("e", NB * BS), ("t0", NB * BS),
                        ("t1", NB * BS), ("w4", NB * HALF), ("d", NB * BS)):
            prep[name] = Dflat[:, at:at + n]
            at += n

        bank = [ctx.enter_context(nc.psum_tensor(f"bank{i}", [P, BANK], F32)) for i in range(BANKS)]

        filled = sem("filled")
        vec_emptied = sem("vec_emptied")
        act_emptied = sem("act_emptied")
        clipped = sem("clipped")
        consts_loaded = sem("consts_loaded")
        prep_loaded = sem("prep_loaded")
        prep_step = sem("prep_step")
        prep_product = sem("prep_product")
        prep_stored = sem("prep_stored")
        weights_loaded = {n: sem(f"weights_loaded{n}") for n in (0, 2, 3)}
        weights_signed = sem("weights_signed")
        tables_loaded = sem("tables_loaded")
        l1_weights_loaded = sem("l1_weights_loaded")
        x_loaded = [sem(f"x_loaded{t}") for t in range(NT)]
        other_loaded = [sem(f"other_loaded{t}") for t in range(NT)]
        mixed = [sem(f"mixed{t}") for t in range(NT)]
        summed = [sem(f"summed{t}") for t in range(NT)]
        stored = [sem(f"stored{t}") for t in range(NT)]
        pads_written = sem("pads_written")
        flipped_loaded = [sem(f"flipped_loaded{n}") for n in range(2)]

        def rows(a):
            return a.rearrange("(h p) c -> p h c", p=P)

        class Pass:

            def __init__(self, layer, plan, fills, vec, act):
                self.layer, self.plan = layer, plan
                self.fills, self.vec, self.act = fills, vec + 1, act + 1
                self.scale_in = 1.0 if layer in (0, 1) else 1.0 / H
                self.scale_out = {0: 1.0 / TOK, 1: 2.0 / (B * TOK * C)}.get(layer, 1.0 / H)
                self.inv_h = cst("inv_h_dht" if layer == 1 else "inv_h")
                self.inv_w = cst("inv_w_dht" if layer == 1 else "inv_w")

            def bank(self, key):
                return bank[self.plan.unit[key] % BANKS]

            def fill_of(self, key):
                return self.fills + self.plan.unit[key] + 1

            def wait_filled(self, eng, key):
                eng.wait_ge(filled, self.fill_of(key))

            def wait_emptied(self, eng, key):
                if self.plan.by[key] == "vec":
                    eng.wait_ge(vec_emptied, self.vec + self.plan.emptied[key])
                else:
                    eng.wait_ge(act_emptied, self.act + self.plan.emptied[key])

            def wait_bank(self, pe, key):
                n = self.plan.unit[key] - BANKS
                if n >= 0:
                    self.wait_emptied(pe, self.plan.order[n])

            def wait_both(self, eng, stage, t, last):
                self.wait_emptied(eng, (stage, t, last - 1))
                self.wait_emptied(eng, (stage, t, last))

        def pass_l0(i):
            return Pass(0, conv, i * conv.fills, i * conv.vec, i * conv.act)

        def pass_l1(i):
            return Pass(1, dht, i * dht.fills + 2 * conv.fills, i * dht.vec + 2 * conv.vec,
                        i * dht.act + 2 * conv.act)

        def pass_l23(i, layer):
            n = layer - 2
            return Pass(layer, conv, i * (2 * conv.fills) + (2 * conv.fills + 2 * dht.fills + n * conv.fills),
                        i * (2 * conv.vec) + (2 * conv.vec + 2 * dht.vec + n * conv.vec),
                        i * (2 * conv.act) + (2 * conv.act + 2 * dht.act + n * conv.act))

        def clips_before(i, layer):
            if layer == 0:
                return i * STEPS
            if layer == 1:
                return i * PAIRS + 2 * STEPS
            return i * (2 * STEPS) + (2 * STEPS + 2 * PAIRS + (layer - 2) * STEPS)

        block = ctx.enter_context(nc.Block())

        @block.sync
        def _(sp):
            sp.dma_start(const[:, :], consts).then_inc(consts_loaded, 16)

            def load_weights(layer, n):
                w3, w4, bias = weights(layer)
                sp.dma_start(w3, conv_w3[n]).then_inc(weights_loaded[layer], 16)
                sp.dma_start(w4[0:MROWS], conv_w4[n]).then_inc(weights_loaded[layer], 16)
                sp.dma_start(bias[0:MROWS], conv_bias[n]).then_inc(weights_loaded[layer], 16)

            def load_x(src, t, stores):
                if not isinstance(stores, int) or stores > 0:
                    sp.wait_ge(stored[t], 16 * stores)
                sp.dma_start(X[:, t], rows(src)[:, :, t * P:(t + 1) * P]).then_inc(x_loaded[t], 16)

            def load_other(src, t, before):
                if t == 0:
                    sp.wait_ge(filled, before - TAIL)
                sp.dma_start(Dflat[:, t * HP * P:(t + 1) * HP * P].rearrange("p (h c) -> p h c", c=P),
                             rows(src)[:, :, t * P:(t + 1) * P]).then_inc(other_loaded[t], 16)

            load_weights(0, 0)
            for image in range(B):
                for t in range(NT):
                    load_x(x[image], t, image)

            sp.wait_ge(filled, 2 * conv.fills)
            sp.dma_start(tables[:, 0:2 * NT * C], fwd_c_dram).then_inc(tables_loaded, 16)
            sp.dma_start(tables[:, 2 * NT * C:], inv_c_dram).then_inc(tables_loaded, 16)
            sp.wait_ge(prep_stored, 48)
            with sp.Fori(0, B) as i:
                p = pass_l1(i)
                for t in range(NT):
                    load_x(after_l0[0], t, i + B)
                    load_other(after_l0[1], t, p.fills)
                p.wait_filled(sp, ("T1", NT - 1, T1_UNITS - 1))
                sp.dma_start(w3_l1[0:MROWS].rearrange("p b r -> p (b r)"), l1_first).then_inc(l1_weights_loaded, 16)
                sp.dma_start(w4_l1[0:MROWS].rearrange("p b r -> p (b r)"), l1_second).then_inc(l1_weights_loaded, 16)
                image = after_l0[i].rearrange("(h w) c -> h w c", w=W)
                for m in range(PAIRS):
                    if m >= 2:
                        p.wait_filled(sp, ("TJ", m - 2, 1))
                    k0, nk = group(m, 2, KW)
                    for k in range(nk):
                        w = (W - k0 - k) % W
                        dst = J[m % 2][k * H:(k + 1) * H, :, HALF:MROWS]
                        src = image[:, w, :].rearrange("h (b c) -> h b c", c=BS)
                        sp.dma_start(dst, src).then_inc(flipped_loaded[m % 2], 16)

            p = pass_l23(0, 2)
            sp.wait_ge(filled, p.fills)
            load_weights(2, 1)
            load_weights(3, 2)
            with sp.Fori(0, B) as i:
                p = pass_l23(i, 2)
                for t in range(NT):
                    load_x(after_l1[0], t, i + 2 * B)
                    load_other(after_l1[1], t, p.fills)

        @block.gpsimd
        def _(pool):
            for n in range(2):
                pool.dma_start(prep[f"v{n}"][0:MROWS], l1_w3[n]).then_inc(prep_loaded, 16)
                pool.dma_start(prep[f"q{n}"][0:BS], l1_q[n]).then_inc(prep_loaded, 16)
                pool.dma_start(prep[f"e{n}"][0:BS], l1_e[n]).then_inc(prep_loaded, 16)
                pool.dma_start(prep[f"t{n}"][0:MROWS], l1_t[n]).then_inc(prep_loaded, 16)
            pool.dma_start(prep["d"][0:BS], l1_e[2]).then_inc(prep_loaded, 16)
            pool.wait_ge(prep_step, PREP_STEPS)
            pool.dma_start(l1_first, prep["v"][0:MROWS]).then_inc(prep_stored, 16)
            pool.dma_start(l1_second, prep["w4"][0:MROWS]).then_inc(prep_stored, 16)
            pool.wait_ge(prep_stored, 32)
            pool.dma_start(l1_first[ONE:ONE + 1], l1_w3_bias).then_inc(prep_stored, 16)

            def store(p, dst):
                for t in range(NT):
                    p.wait_emptied(pool, ("S6", t, INV_UNITS - 1))
                    pool.dma_start(rows(dst)[:, :, t * P:(t + 1) * P], X[:, t]).then_inc(stored[t], 16)

            with pool.Fori(0, B) as i:
                store(pass_l0(i), after_l0[i])
            with pool.Fori(0, B) as i:
                store(pass_l1(i), after_l1[i])
            with pool.Fori(0, B) as i:
                store(pass_l23(i, 3), out[i])
            for t in range(NT):
                pool.wait_ge(stored[t], 16 * 3 * B)

        @block.tensor
        def _(pe):
            def forward(p, x_ready):
                pe.wait_ge(vec_emptied, p.vec)
                pe.wait_ge(act_emptied, p.act)

                def s1(t):
                    x_ready(t)
                    for g in range(S1_UNITS):
                        key = ("S1", t, g)
                        p.wait_bank(pe, key)
                        h0, nh = group(g, S1_GROUP, HP)
                        for k in range(nh):
                            n = 4 * KW
                            mm = nc.tensor.matmul(p.bank(key)[:, k * n:(k + 1) * n], X[:, t, h0 + k], dft_w,
                                                  start=True, stop=True)
                        mm.then_inc(filled, 1)

                def t1(t):
                    p.wait_both(pe, "S1", t, S1_UNITS - 1)
                    for g in range(T1_UNITS):
                        key = ("T1", t, g)
                        p.wait_bank(pe, key)
                        k0, nk = group(g, T_GROUP, KW)
                        for k in range(nk):
                            mm = nc.tensor.transpose(p.bank(key)[:, k * P:(k + 1) * P], A(t)[:, :, k0 + k], identity)
                        mm.then_inc(filled, 1)

                s1(0)
                s1(1)
                t1(0)
                s1(2)
                t1(1)
                t1(2)
                p.wait_both(pe, "T1", NT - 1, T1_UNITS - 1)

            def inverse(p):
                def s5(t):
                    for u in range(INV_UNITS):
                        key = ("S5", t, u)
                        p.wait_bank(pe, key)
                        kws = [0, KW - 1, 1, 2, 3] if u == 0 else range(4 * u, 4 * u + 4)
                        at = 0
                        for k in kws:
                            rhs = p.inv_h[:, 2 * H:3 * H] if k in (0, KW - 1) else p.inv_h[:, 0:2 * H]
                            n = rhs.shape[1]
                            mm = nc.tensor.matmul(p.bank(key)[:, at:at + n], D[:, k, t * P:(t + 1) * P], rhs,
                                                  start=True, stop=True)
                            at += n
                        mm.then_inc(filled, 1)

                def t2(t):
                    p.wait_both(pe, "S5", t, INV_UNITS - 1)
                    for u in range(INV_UNITS):
                        key = ("T2", t, u)
                        p.wait_bank(pe, key)
                        for k in range(T_GROUP):
                            mm = nc.tensor.transpose(p.bank(key)[:, k * P:(k + 1) * P], E(t)[:, :, u * T_GROUP + k],
                                                     identity)
                        mm.then_inc(filled, 1)

                def s6(t):
                    p.wait_both(pe, "T2", t, INV_UNITS - 1)
                    for u in range(INV_UNITS):
                        key = ("S6", t, u)
                        p.wait_bank(pe, key)
                        nc.tensor.matmul(p.bank(key)[:, :], p.inv_w, G(t)[:, u * BANK:(u + 1) * BANK],
                                         start=True, stop=True).then_inc(filled, 1)

                s5(0)
                s5(1)
                t2(0)
                s5(2)
                t2(1)
                s6(0)
                t2(2)
                s6(1)
                s6(2)

            def mlp(p):
                w3, w4, _ = weights(p.layer)

                def s2(n):
                    key = ("S2", n)
                    b, (k0, nk) = n // M_GROUPS, group(n % M_GROUPS, M_GROUP, KW)
                    c0, _ = block_rows(b)
                    p.wait_bank(pe, key)
                    for k in range(nk):
                        for half in range(2):
                            mm = nc.tensor.matmul(
                                p.bank(key)[half * HALF:(half + 1) * HALF, k * H:(k + 1) * H],
                                Bm[:, k0 + k, c0:c0 + HALF], dft_h[:, half * H:(half + 1) * H],
                                start=True, stop=True)
                    mm.then_inc(filled, 1)

                def s3(n):
                    key = ("S3", n)
                    b, (_, nk) = n // M_GROUPS, group(n % M_GROUPS, M_GROUP, KW)
                    p.wait_bank(pe, key)
                    p.wait_emptied(pe, ("S2", n))
                    nc.tensor.matmul(p.bank(key)[0:MROWS, 0:nk * H], w3[:, b], modes[n % 2][:, 0:nk * H],
                                     start=True, stop=True).then_inc(filled, 1)

                def s4(n):
                    key = ("S4", n)
                    b, (_, nk) = n // M_GROUPS, group(n % M_GROUPS, M_GROUP, KW)
                    p.wait_bank(pe, key)
                    p.wait_emptied(pe, ("S3", n))
                    for k in range(nk):
                        for half in range(2):
                            mm = nc.tensor.matmul(
                                p.bank(key)[half * HALF:(half + 1) * HALF, k * BS:(k + 1) * BS],
                                hidden[n % 2][0:MROWS, k * H:(k + 1) * H], w4[0:MROWS, b, half * BS:(half + 1) * BS],
                                start=True, stop=True)
                    mm.then_inc(filled, 1)

                for n in range(STEPS + 2):
                    if n < STEPS:
                        s2(n)
                    if 0 <= n - 1 < STEPS:
                        s3(n - 1)
                    if 0 <= n - 2 < STEPS:
                        s4(n - 2)
                p.wait_emptied(pe, ("S4", STEPS - 1))

            def hartley(p, i):
                def f2(m):
                    k0, nk = group(m, 2, KW)
                    for k in range(nk):
                        key = ("F2", m, k)
                        p.wait_bank(pe, key)
                        for t in range(NT):
                            mm = nc.tensor.matmul(p.bank(key)[:, t * P:(t + 1) * P], Bm[:, k0 + k, t * P:(t + 1) * P],
                                                  dft_h_uv, start=True, stop=True)
                        mm.then_inc(filled, 1)

                def cf(m):
                    key, nk = ("CF", m), group(m, 2, KW)[1]
                    p.wait_bank(pe, key)
                    p.wait_emptied(pe, ("F2", m, nk - 1))
                    for a in range(2 * NT):
                        mm = nc.tensor.matmul(p.bank(key)[0:nk * H, 0:C], UV[:, a, 0:nk * H], fwd_c[:, a],
                                              start=a == 0, stop=a == 2 * NT - 1)
                    mm.then_inc(filled, 1)

                def tj(m):
                    p.wait_emptied(pe, ("CF", m))
                    columns = [sum(group(n, 2, KW)[1] for n in range(m % 2, end, 2)) for end in (m + 1, PAIRS)]
                    pe.wait_ge(flipped_loaded[m % 2], i * (16 * columns[1]) + 16 * columns[0])
                    for half in range(2):
                        key = ("TJ", m, half)
                        p.wait_bank(pe, key)
                        for b in range(4):
                            mm = nc.tensor.transpose(p.bank(key)[0:MROWS, b * P:(b + 1) * P], J[m % 2][:, half * 4 + b],
                                                     identity)
                        mm.then_inc(filled, 1)

                def h1(m):
                    nk = group(m, 2, KW)[1]
                    for half in range(2):
                        key = ("H1", m, half)
                        p.wait_bank(pe, key)
                        p.wait_emptied(pe, ("TJ", m, half))
                        for b in range(4):
                            mm = nc.tensor.matmul(p.bank(key)[0:MROWS, b * P:b * P + nk * H],
                                                  w3_l1[0:MROWS, half * 4 + b], pair[half][0:MROWS, b * P:b * P + nk * H],
                                                  start=True, stop=True)
                        mm.then_inc(filled, 1)

                def h2(m):
                    key, nk = ("H2", m), group(m, 2, KW)[1]
                    p.wait_bank(pe, key)
                    p.wait_emptied(pe, ("H1", m, 1))
                    for b in range(NB):
                        row, g = b % 2 * HALF, b // 2
                        mm = nc.tensor.matmul(p.bank(key)[row:row + HALF, g * P:g * P + nk * H], w4_l1[0:MROWS, b],
                                              hid[b // 4][0:MROWS, b % 4 * P:b % 4 * P + nk * H],
                                              start=True, stop=True)
                    mm.then_inc(filled, 1)

                def ci(m):
                    p.wait_emptied(pe, ("H2", m))
                    for k in range(group(m, 2, KW)[1]):
                        key = ("CI", m, k)
                        p.wait_bank(pe, key)
                        for g in range(NB // 2):
                            for half in range(2):
                                mm = nc.tensor.matmul(
                                    p.bank(key)[half * HALF:(half + 1) * HALF, 0:C],
                                    shrunk[m % 2][:, g * P + k * H:g * P + (k + 1) * H], inv_c[:, g, half],
                                    start=g == 0, stop=g == NB // 2 - 1)
                        mm.then_inc(filled, 1)

                f2(0)
                pe.wait_ge(tables_loaded, 32)
                cf(0)
                pe.wait_ge(pads_written, i * 2 + 2)
                pe.wait_ge(l1_weights_loaded, i * 32 + 32)
                for m in range(PAIRS):
                    tj(m)
                    if m + 1 < PAIRS:
                        f2(m + 1)
                    h1(m)
                    if m + 1 < PAIRS:
                        cf(m + 1)
                    h2(m)
                    if m > 0:
                        ci(m - 1)
                ci(PAIRS - 1)
                p.wait_emptied(pe, ("CI", PAIRS - 1, group(PAIRS - 1, 2, KW)[1] - 1))

            pe.wait_ge(prep_step, PREP_OPERANDS)
            for b in range(NB):
                mm = nc.tensor.matmul(bank[BANKS - 1][0:MROWS, b * BS:(b + 1) * BS],
                                      prep["q"][0:BS, b * MROWS:(b + 1) * MROWS], prep["e"][0:BS, b * BS:(b + 1) * BS],
                                      start=True, stop=True)
            mm.then_inc(prep_product, 1)
            pe.wait_ge(consts_loaded, 16)
            pe.wait_ge(weights_signed, 2)
            pe.wait_ge(prep_step, PREP_STEPS)

            with pe.Fori(0, B) as i:
                p = pass_l0(i)
                forward(p, lambda t: pe.wait_ge(x_loaded[t], i * 16 + 16))
                mlp(p)
                inverse(p)
            with pe.Fori(0, B) as i:
                p = pass_l1(i)
                forward(p, lambda t: pe.wait_ge(mixed[t], i + 1))
                hartley(p, i)
                inverse(p)
            pe.wait_ge(weights_signed, 6)
            with pe.Fori(0, B) as i:
                for layer in (2, 3):
                    p = pass_l23(i, layer)
                    forward(p, lambda t: pe.wait_ge(mixed[t], i + (B + 1)))
                    mlp(p)
                    inverse(p)

        def empty_forward(p, eng, me, copy, emptied):
            for key in p.plan.order:
                if key[0] not in ("S1", "T1") or p.plan.by[key] != me:
                    continue
                stage, t, g = key
                p.wait_filled(eng, key)
                if stage == "S1":
                    h0, nh = group(g, S1_GROUP, HP)
                    dst = A(t)[:, :, :].rearrange("p (a h) k -> p h a k", h=HP)[:, h0:h0 + nh]
                    src = p.bank(key)[:, 0:nh * 4 * KW].rearrange("p (h a k) -> p h a k", a=4, k=KW)
                else:
                    k0, nk = group(g, T_GROUP, KW)
                    dst = Bm[:, k0:k0 + nk, t * P:(t + 1) * P]
                    src = p.bank(key)[:, 0:nk * P].rearrange("p (k c) -> p k c", c=P)
                copy(dst, src).then_inc(emptied, 1)

        def empty_inverse(p, eng, me, copy, emptied):
            for key in p.plan.order:
                if key[0] not in ("S5", "T2", "S6") or p.plan.by[key] != me:
                    continue
                stage, t, u = key
                p.wait_filled(eng, key)
                if stage == "S5":
                    dst = E(t).rearrange("p (j q) h -> p q j h", j=2)[:, 8 * u:8 * u + 8]
                    copy(dst, p.bank(key)[:, :].rearrange("p (q j h) -> p q j h", j=2, h=HP)).then_inc(emptied, 1)
                elif stage == "T2":
                    copy(G(t)[:, u * BANK:(u + 1) * BANK], p.bank(key)[:, :]).then_inc(emptied, 1)
                else:
                    rows4 = X[:, t, 4 * u:4 * u + 4].rearrange("p h c -> p (h c)")
                    nc.vector.scalar_tensor_tensor(out=rows4, in0=p.bank(key)[:, :], scalar=p.scale_out, in1=rows4,
                                                   op0=ALU.mult, op1=ALU.add).then_inc(emptied, 1)

        @block.scalar
        def _(act):
            def copy(dst, src):
                return nc.scalar.activation(dst, src, ACT.Copy)

            def mlp(p):
                _, _, bias = weights(p.layer)
                for n in range(STEPS + 1):
                    if n < STEPS:
                        cols = group(n % M_GROUPS, M_GROUP, KW)[1] * H
                        key = ("S2", n)
                        p.wait_filled(act, key)
                        nc.scalar.activation(modes[n % 2][:, 0:cols], p.bank(key)[:, 0:cols], ACT.Copy,
                                             scale=p.scale_in).then_inc(act_emptied, 1)
                    if n > 0:
                        cols = group((n - 1) % M_GROUPS, M_GROUP, KW)[1] * H
                        key, b = ("S3", n - 1), (n - 1) // M_GROUPS
                        p.wait_filled(act, key)
                        nc.scalar.activation(hidden[(n - 1) % 2][0:MROWS, 0:cols], p.bank(key)[0:MROWS, 0:cols],
                                             ACT.Relu, bias=bias[0:MROWS, b:b + 1]).then_inc(act_emptied, 1)

            def hartley(p):
                def f2(m):
                    for k in range(group(m, 2, KW)[1]):
                        key = ("F2", m, k)
                        p.wait_filled(act, key)
                        copy(UV[:, :, k * H:(k + 1) * H],
                             p.bank(key)[:, 0:C].rearrange("p (a n) -> p a n", n=H)).then_inc(act_emptied, 1)

                f2(0)
                for m in range(PAIRS):
                    n = group(m, 2, KW)[1] * H
                    for half in range(2):
                        key = ("TJ", m, half)
                        p.wait_filled(act, key)
                        copy(pair[half][0:MROWS].rearrange("p (b n) -> p b n", n=P)[:, :, 0:n],
                             p.bank(key)[0:MROWS].rearrange("p (b n) -> p b n", n=P)[:, :, 0:n]).then_inc(act_emptied, 1)
                    if m + 1 < PAIRS:
                        f2(m + 1)
                    for half in range(2):
                        key = ("H1", m, half)
                        p.wait_filled(act, key)
                        nc.scalar.activation(hid[half][0:MROWS].rearrange("p (b n) -> p b n", n=P)[:, :, 0:n],
                                             p.bank(key)[0:MROWS].rearrange("p (b n) -> p b n", n=P)[:, :, 0:n],
                                             ACT.Relu).then_inc(act_emptied, 1)

            act.wait_ge(vec_emptied, 1)
            nc.scalar.activation(warm[:, 1:2], warm[:, 0:1], ACT.Relu).then_inc(act_emptied, 1)
            act.wait_ge(weights_loaded[0], 48)
            with act.Fori(0, B) as i:
                p = pass_l0(i)
                empty_forward(p, act, "act", copy, act_emptied)
                mlp(p)
                empty_inverse(p, act, "act", copy, act_emptied)
            with act.Fori(0, B) as i:
                p = pass_l1(i)
                empty_forward(p, act, "act", copy, act_emptied)
                hartley(p)
                empty_inverse(p, act, "act", copy, act_emptied)
            act.wait_ge(weights_loaded[2], 48)
            act.wait_ge(weights_loaded[3], 48)
            with act.Fori(0, B) as i:
                for layer in (2, 3):
                    p = pass_l23(i, layer)
                    empty_forward(p, act, "act", copy, act_emptied)
                    mlp(p)
                    empty_inverse(p, act, "act", copy, act_emptied)

        @block.vector
        def _(vec):
            def copy(dst, src):
                return nc.vector.tensor_copy(dst, src)

            def shrink(p, key, dst, src, held, clips, done):
                p.wait_filled(vec, key)
                if done is not None:
                    vec.wait_ge(vec_emptied, p.vec + done)
                nc.vector.tensor_scalar(held, src, -LAMBDA, LAMBDA, ALU.max, ALU.min).then_inc(clipped, 1)
                vec.wait_ge(clipped, clips)
                nc.vector.tensor_tensor(dst, src, held, ALU.subtract).then_inc(vec_emptied, 1)

            def mlp(p, i):
                clips = clips_before(i, p.layer)
                for n in range(STEPS):
                    key, b = ("S4", n), n // M_GROUPS
                    k0, nk = group(n % M_GROUPS, M_GROUP, KW)
                    src = p.bank(key)[:, 0:nk * BS].rearrange("p (k c) -> p k c", c=BS)
                    held = clip[n % 2][:, 0:nk * BS].rearrange("p (k c) -> p k c", c=BS)
                    shrink(p, key, D[:, k0:k0 + nk, b * BS:(b + 1) * BS], src, held, clips + (n + 1),
                           p.plan.emptied[("S4", n - 2)] if n >= 2 else None)

            def hartley(p, i):
                clips = clips_before(i, 1)
                p.wait_filled(vec, ("T1", NT - 1, T1_UNITS - 1))
                both = ring[:, 2 * NT * P:2 * NT * P + 2 * NB * MROWS].rearrange("p (b r) -> p b r", r=MROWS)
                nc.vector.memset(both[:, :, ONE:ONE + 1], 1.0).then_inc(pads_written, 1)
                nc.vector.memset(both[:, :, ONE + 1:HALF], 0.0).then_inc(pads_written, 1)

                def cf(m):
                    key, n = ("CF", m), group(m, 2, KW)[1] * H
                    p.wait_filled(vec, key)
                    copy(J[m % 2][0:n, :, 0:BS],
                         p.bank(key)[0:n, 0:C].rearrange("p (b c) -> p b c", c=BS)).then_inc(vec_emptied, 1)

                def ci(m):
                    k0, nk = group(m, 2, KW)
                    for k in range(nk):
                        key = ("CI", m, k)
                        p.wait_filled(vec, key)
                        copy(D[:, k0 + k], p.bank(key)[:, 0:C]).then_inc(vec_emptied, 1)

                cf(0)
                for m in range(PAIRS):
                    if m + 1 < PAIRS:
                        cf(m + 1)
                    key, n = ("H2", m), group(m, 2, KW)[1] * H
                    src, held, dst = (v.rearrange("p (g n) -> p g n", n=P)[:, :, 0:n]
                                      for v in (p.bank(key)[:, :], clip_l1, shrunk[m % 2]))
                    shrink(p, key, dst, src, held, clips + (m + 1), p.plan.emptied[("H2", m - 1)] if m else None)
                    if m > 0:
                        ci(m - 1)
                ci(PAIRS - 1)

            def mix(i, n, halve):
                for t in range(NT):
                    tile = X[:, t].rearrange("p h c -> p (h c)")
                    other = Dflat[:, t * HP * P:(t + 1) * HP * P]
                    vec.wait_ge(x_loaded[t], (i + (B * n + 1)) * 16)
                    vec.wait_ge(other_loaded[t], (i + (B * (n - 1) + 1)) * 16)
                    whole = mixed[t] if not halve else summed[t]
                    nc.vector.scalar_tensor_tensor(out=tile, in0=other, scalar=sign[:, bass.ds(i, 1)], in1=tile,
                                                   op0=ALU.mult, op1=ALU.add).then_inc(whole, 1)
                    if halve:
                        vec.wait_ge(summed[t], i + 1)
                        nc.vector.tensor_scalar(tile, tile, 0.5, None, ALU.mult).then_inc(mixed[t], 1)

            def flip_sign(layer):
                w3, w4, _ = weights(layer)
                vec.wait_ge(weights_loaded[layer], 48)
                nc.vector.tensor_scalar(w3[HALF:P, :, 0:BS], w3[HALF:P, :, 0:BS], -1.0, None,
                                        ALU.mult).then_inc(weights_signed, 1)
                nc.vector.tensor_scalar(w4[HALF:MROWS, :, 0:BS], w4[HALF:MROWS, :, 0:BS], -1.0, None,
                                        ALU.mult).then_inc(weights_signed, 1)

            nc.vector.memset(warm[:, 0:1], 0.0).then_inc(vec_emptied, 1)
            flip_sign(0)

            steps = 0

            def step(ins):
                nonlocal steps
                steps += 1
                ins.then_inc(prep_step, 1)

            def after_steps():
                vec.wait_ge(prep_step, steps)

            def blocks(name, r):
                return prep[name].rearrange("p (b r) -> p b r", r=r)

            vec.wait_ge(prep_loaded, 9 * 16)
            q0, q1, q = (blocks(n, MROWS) for n in ("q0", "q1", "q"))
            step(nc.vector.tensor_tensor(q[0:BS, :, 0:HALF], q0[0:BS, :, 0:HALF], q1[0:BS, :, 0:HALF], ALU.add))
            step(nc.vector.tensor_tensor(q[0:BS, :, HALF:], q0[0:BS, :, HALF:], q1[0:BS, :, HALF:], ALU.subtract))
            step(nc.vector.tensor_tensor(prep["e"][0:BS], prep["e0"][0:BS], prep["e1"][0:BS], ALU.subtract))
            after_steps()
            step(nc.vector.tensor_scalar(q[0:BS, :, 0:BS], q[0:BS, :, 0:BS], 0.5, None, ALU.mult))
            step(nc.vector.tensor_scalar(q[0:BS, :, HALF:], q[0:BS, :, HALF:], 0.5, None, ALU.mult))
            step(nc.vector.scalar_tensor_tensor(out=prep["e"][0:BS], in0=prep["e"][0:BS], scalar=0.5,
                                                in1=prep["d"][0:BS], op0=ALU.mult, op1=ALU.add))
            v0, v1, v = (blocks(n, MROWS) for n in ("v0", "v1", "v"))
            for rows_, first in ((slice(0, HALF), ALU.add), (slice(HALF, MROWS), ALU.subtract)):
                second = ALU.subtract if first == ALU.add else ALU.add
                step(nc.vector.tensor_tensor(v[rows_, :, 0:HALF], v0[rows_, :, 0:HALF], v1[rows_, :, 0:HALF], first))
                step(nc.vector.tensor_tensor(v[rows_, :, HALF:], v0[rows_, :, HALF:], v1[rows_, :, HALF:], second))
            after_steps()
            assert steps == PREP_OPERANDS
            step(nc.vector.tensor_scalar(prep["v"][0:MROWS], prep["v"][0:MROWS], 0.5, None, ALU.mult))
            t0, t1 = prep["t0"], prep["t1"]
            step(nc.vector.tensor_tensor(t0[0:MROWS], t0[0:MROWS], t1[0:MROWS], ALU.add))
            step(nc.vector.memset(prep["w4"][0:MROWS], 0.0))
            after_steps()
            step(nc.vector.tensor_scalar(t0[HALF:MROWS], t0[HALF:MROWS], 0.5, None, ALU.mult))
            after_steps()
            vec.wait_ge(prep_product, 1)
            step(nc.vector.tensor_tensor(
                blocks("w4", HALF)[0:MROWS, :, 0:BS],
                bank[BANKS - 1][0:MROWS, 0:NB * BS].rearrange("p (b c) -> p b c", c=BS),
                blocks("t0", BS)[0:MROWS], ALU.add))
            assert steps == PREP_STEPS
            vec.wait_ge(prep_stored, 48)

            with vec.Fori(0, B) as i:
                p = pass_l0(i)
                empty_forward(p, vec, "vec", copy, vec_emptied)
                mlp(p, i)
                empty_inverse(p, vec, "vec", copy, vec_emptied)
            with vec.Fori(0, B) as i:
                p = pass_l1(i)
                mix(i, 1, False)
                empty_forward(p, vec, "vec", copy, vec_emptied)
                hartley(p, i)
                empty_inverse(p, vec, "vec", copy, vec_emptied)
            flip_sign(2)
            flip_sign(3)
            with vec.Fori(0, B) as i:
                mix(i, 2, True)
                for layer in (2, 3):
                    p = pass_l23(i, layer)
                    empty_forward(p, vec, "vec", copy, vec_emptied)
                    mlp(p, i)
                    empty_inverse(p, vec, "vec", copy, vec_emptied)


def lay_out_conv(w1, b1, w2, b2):
    w3 = np.zeros((P, NB, MROWS), np.float32)
    w4 = np.zeros((MROWS, NB, 2 * BS), np.float32)
    bias = np.zeros((MROWS, NB), np.float32)
    for b in range(NB):
        at = block_rows(b)[1]
        for rows, first, second in ((at, 0, 1), (HALF + at, 1, 0)):
            w3[rows:rows + BS, b, 0:BS] = w1[first, b]
            w3[rows:rows + BS, b, HALF:] = w1[second, b]
        for rows, first, second in ((0, 0, 1), (HALF, 1, 0)):
            w4[rows:rows + BS, b, 0:BS] = w2[first, b]
            w4[rows:rows + BS, b, BS:] = w2[second, b]
            bias[rows:rows + BS, b] = b1[first, b]
        w4[ONE, b, 0:BS], w4[ONE, b, BS:] = b2[0, b], b2[1, b]
    bias[ONE] = 1.0
    return w3, w4, bias


def lay_out_hartley(w1, b1, w2, b2):
    first = np.zeros((2, MROWS, NB, MROWS), np.float32)
    first_bias = np.zeros((1, NB, MROWS), np.float32)
    q = np.zeros((2, BS, NB, MROWS), np.float32)
    e = np.zeros((3, BS, NB, BS), np.float32)
    t = np.zeros((2, MROWS, NB, BS), np.float32)
    for b in range(NB):
        for n in range(2):
            for r in (0, HALF):
                for c in (0, HALF):
                    first[n, r:r + BS, b, c:c + BS] = w1[n, b]
                q[n, :, b, r:r + BS] = w2[n, b].T
            e[n, :, b] = w2[n, b]
            t[n, HALF:, b] = w2[n, b]
        first_bias[0, b, 0:BS], first_bias[0, b, HALF:] = b1[0, b], b1[1, b]
        first_bias[0, b, ONE] = 1.0
        q[0, :, b, ONE] = b2[0, b]
        t[0, ONE, b] = b2[1, b]
        e[2, :, b] = np.eye(BS)
    return first, first_bias, q, e, t


def kernel(x, **weights):
    import concourse.bacc as bacc
    from concourse import mybir
    from concourse.bass_utils import run_bass_kernel_spmd

    w = {n: np.asarray(a) for n, a in weights.items()}
    for n in ("L2_conv_w1", "L2_conv_b1", "L2_conv_w2", "L2_conv_b2"):
        w[n] = np.moveaxis(w[n], -1, 0)
    layers = {n: [w[f"L{n}_conv_{k}"] for k in ("w1", "b1", "w2", "b2")] for n in range(4)}
    laid = [lay_out_conv(*layers[n]) for n in (0, 2, 3)]
    first, first_bias, q, e, t = lay_out_hartley(*layers[1])
    parts, fwd_c, inv_c = constants()
    const_at, at = {}, 0
    for name, a in parts.items():
        const_at[name] = (at, a.shape[1])
        at += a.shape[1]
    arrays = {
        "x": np.asarray(x).reshape(B, TOK, C),
        "consts": np.concatenate(list(parts.values()), 1),
        "fwd_c": fwd_c,
        "inv_c": inv_c,
        "conv_w3": np.stack([a[0] for a in laid]),
        "conv_w4": np.stack([a[1] for a in laid]),
        "conv_bias": np.stack([a[2] for a in laid]),
        "l1_w3": first.reshape(2, MROWS, -1),
        "l1_w3_bias": first_bias.reshape(1, -1),
        "l1_q": q.reshape(2, BS, -1),
        "l1_e": e.reshape(3, BS, -1),
        "l1_t": t.reshape(2, MROWS, -1),
    }
    arrays = {n: np.ascontiguousarray(a) for n, a in arrays.items()}
    nc = bacc.Bacc("TRN2", target_bir_lowering=False, num_devices=1)
    ins = [nc.dram_tensor(n, a.shape, mybir.dt.float32, kind="ExternalInput").ap() for n, a in arrays.items()]
    out = nc.dram_tensor("out", (B, TOK, C), mybir.dt.float32, kind="ExternalOutput").ap()
    build(nc, *ins, out, const_at)
    r = run_bass_kernel_spmd(nc, [arrays], core_ids=[0])
    return r.results[0]["out"].reshape(B, H, W, C)
```

```python
import numpy as np

B, H, W, C = 2, 64, 64, 384
NB = 8
BS = C // NB
P = 128
NT = C // P
HP = H // 2
KW = W // 2 + 1
Q = 64
TOK = H * W
BANK = 512
BANKS = 8
ONE = BS
HALF = 64
MROWS = HALF + BS
LAMBDA = 0.01

S1_GROUP = 3
S1_UNITS = -(-HP // S1_GROUP)
T_GROUP = BANK // P
T1_UNITS = -(-KW // T_GROUP)
M_GROUP = BANK // H
M_GROUPS = -(-KW // M_GROUP)
STEPS = NB // 2 * M_GROUPS
TB = BS // NT
INV_UNITS = Q * H // BANK
PAIRS = -(-KW // 2)
EVEN = C // 2 + 1
MIDDLE = P // 2 + 1
PREP_OPERANDS, PREP_STEPS = 10, 15
TAIL = 5 * INV_UNITS


def group(n, size, total):
    return n * size, min(size, total - n * size)


def forward_order():
    s1 = [[("S1", t, g) for g in range(S1_UNITS)] for t in range(NT)]
    t1 = [[("T1", t, g) for g in range(T1_UNITS)] for t in range(NT)]
    return s1[0] + s1[1] + t1[0] + s1[2] + t1[1] + t1[2]


def inverse_order():
    s5, t2, s6 = ([[(s, t, u) for u in range(INV_UNITS)] for t in range(NT)] for s in ("S5", "T2", "S6"))
    return s5[0] + s5[1] + t2[0] + s5[2] + t2[1] + s6[0] + t2[2] + s6[1] + s6[2]


def s2_units(n):
    return -(-group(n % M_GROUPS, M_GROUP, KW)[1] // T_GROUP)


def conv_order():
    mid = []
    for n in range(STEPS + 2):
        if n < STEPS:
            mid += [("S2", n, u) for u in range(s2_units(n))]
        for lag, s in ((1, "S3"), (2, "S4")):
            if 0 <= n - lag < STEPS:
                mid += [(s, n - lag, 0), (s, n - lag, 1)]
    return forward_order() + mid + inverse_order()


def hartley_order():
    def cols(m):
        return range(group(m, 2, KW)[1])
    mid = [("F2", 0, k) for k in cols(0)] + [("CF", 0)]
    for m in range(PAIRS):
        mid += [("TJ", m, 0), ("TJ", m, 1)]
        if m + 1 < PAIRS:
            mid += [("F2", m + 1, k) for k in cols(m + 1)]
        mid += [("H1", m, 0), ("H1", m, 1)]
        if m + 1 < PAIRS:
            mid += [("CF", m + 1)]
        mid += [("H2", m)]
        if m > 0:
            mid += [("CI", m - 1, "even"), ("CI", m - 1, "odd")]
    mid += [("CI", PAIRS - 1, "even"), ("CI", PAIRS - 1, "odd")]
    return forward_order() + mid + inverse_order()


class Counts:

    VECTOR = {"S4", "S6", "CF", "H2", ("CI", "odd")}
    SCALAR = {"S2", "S3", "F2", "TJ", "H1", ("CI", "even")}

    def __init__(self, order):
        self.order = order
        self.unit, self.by, self.emptied = {}, {}, {}
        self.vec = self.act = 0
        for n, key in enumerate(order):
            self.unit[key] = n
            kinds = {key[0], (key[0], key[-1])}
            self.by[key] = ("vec" if kinds & self.VECTOR else "act" if kinds & self.SCALAR
                            else ("vec", "act")[key[2] % 2])
            if self.by[key] == "vec":
                self.vec += 1
                self.emptied[key] = self.vec
            else:
                self.act += 1
                self.emptied[key] = self.act
        self.fills = len(order)


def slots():
    return np.array([NT * m + t for t in range(NT) for m in range(TB)])


def constants():
    def cos(a, n):
        return np.cos(2 * np.pi * (a % n) / n).round(17) + 0.0

    def sin(a, n):
        a = a % n
        s = np.sin(2 * np.pi * a / n)
        return np.where((2 * a) % n == 0, 0.0, s)

    k64, h64 = np.arange(64), np.arange(64)
    kw = np.arange(KW)
    cw, sw = cos(np.outer(h64, kw), 64), sin(np.outer(h64, kw), 64)
    dft_w = np.zeros((2, W, 2, 2, KW))
    for j in range(2):
        dft_w[j, :, 0, j] = cw
        dft_w[j, :, 1, j] = -sw
    rows = np.array([2 * hp + j for j in range(2) for hp in range(HP)])
    ch, sh = cos(np.outer(rows, k64), 64), sin(np.outer(rows, k64), 64)
    re, im = np.concatenate([ch, sh]), np.concatenate([-sh, ch])
    dft_h = np.concatenate([re, im], 1)
    flip = -k64 % 64
    dft_h_uv = np.concatenate([(re + im)[:, flip], (im - re)[:, flip]], 1)
    ch, sh = ch.T, sh.T
    zr, zi = np.concatenate([ch, -sh]), np.concatenate([sh, ch])
    inv_h = np.concatenate([zr, zi, zr], 1)
    ch, sh = ch[flip], sh[flip]
    zr, zi = np.concatenate([ch, sh]), np.concatenate([-sh, ch])
    inv_h_dht = np.concatenate([zr, zi, zr + zi], 1)
    inv_w, inv_w_dht = np.zeros((2, 2, Q, 2, W))
    cw, sw = cw.T, sw.T
    for j in range(2):
        for q, k in ((0, 0), (1, 32)):
            inv_w[j, q, j] = cw[k]
            inv_w_dht[j, q, j] = cw[k]
        for k in range(1, 32):
            inv_w[j, 2 * k, j] = 2 * cw[k]
            inv_w[j, 2 * k + 1, j] = -2 * sw[k]
            inv_w_dht[j, 2 * k, j] = cw[k] - sw[k]
            inv_w_dht[j, 2 * k + 1, j] = cw[k] + sw[k]
    tile_c = (NT * np.arange(P)[None, :] + np.arange(NT)[:, None]).ravel()
    block_c = (BS * np.arange(NB)[:, None] + slots()[None, :]).ravel()
    odd = np.zeros(C, bool)
    odd[P // 2 + 1:P], odd[2 * P:] = True, True
    cc = np.outer(tile_c, block_c)
    fwd_c = np.where(odd[:, None], sin(-cc, C), cos(cc, C)).reshape(NT, P, C).transpose(1, 0, 2)
    inv = np.where(odd[:, None], -sin(cc, C), cos(cc, C)).T
    inv = np.concatenate([inv[:, ~odd], inv[:, odd]], 1)
    inv_c = np.zeros((2, HALF, NB // 2, C))
    for b in range(NB):
        inv_c[b % 2, :BS, b // 2] = inv[b * BS:(b + 1) * BS]
    parts = {"identity": np.eye(P), "dft_w": dft_w, "dft_h": dft_h, "dft_h_uv": dft_h_uv, "inv_h": inv_h,
             "inv_h_dht": inv_h_dht, "inv_w": inv_w, "inv_w_dht": inv_w_dht}
    parts = {n: a.reshape(P, -1).astype(np.float32) for n, a in parts.items()}
    return parts, fwd_c.reshape(P, -1).astype(np.float32), inv_c.reshape(P, -1).astype(np.float32)


def build(nc, x, consts, fwd_c_dram, inv_c_dram, conv_w3, conv_w4, conv_bias, l1_w3, l1_w3_bias, l1_q, l1_e, l1_t,
          out, const_at):
    import concourse.bass as bass
    from concourse import mybir
    from contextlib import ExitStack

    F32 = mybir.dt.float32
    ALU = mybir.AluOpType
    ACT = mybir.ActivationFunctionType
    conv, dht = Counts(conv_order()), Counts(hartley_order())

    ctx = ExitStack()
    with ctx:
        def sb(name, shape):
            return ctx.enter_context(nc.sbuf_tensor(name, shape, F32))

        def sem(name):
            return ctx.enter_context(nc.semaphore(name))

        def dram(name, shape):
            return nc.dram_tensor(name, shape, F32, kind="Internal").ap()

        after_l0 = dram("after_l0", (B, TOK, C))
        l1_sum = dram("l1_sum", (TOK, C))
        second_in = dram("second_in", (TOK, C))
        l1_first = dram("l1_first", (MROWS, NB * MROWS))
        l1_second = dram("l1_second", (MROWS, NB * HALF))

        X = sb("X", [P, NT, HP, P])
        mid = sb("mid", [P, NB * HALF * KW])
        D = sb("D", [P, KW, C])
        ring = sb("ring", [P, 2 * P * KW])
        const = sb("const", [P, consts.shape[1]])

        Bpad = mid[:, 0:NB * HALF * KW].rearrange("p (k b s) -> p k b s", b=NB, s=HALF)
        Bpair = mid[:, 0:NB * HALF * KW].rearrange("p (k a n) -> p k a n", a=NB // 2, n=P)
        Bm = mid[:, 0:KW * C].rearrange("p (k c) -> p k c", c=C)
        tables = mid[:, KW * C:KW * C + (NT + NB // 2) * C]

        warm = sb("warm", [P, 2])

        def cst(name):
            at, n = const_at[name]
            return const[:, at:at + n]

        identity, dft_w, dft_h, dft_h_uv = (cst(n) for n in ("identity", "dft_w", "dft_h", "dft_h_uv"))

        def A(t):
            return ring[:, (t % 2) * P * KW:(t % 2 + 1) * P * KW].rearrange("p (r k) -> p r k", k=KW)

        def E(t):
            at = (t % 2) * P * HP
            return ring[:, at:at + P * HP].rearrange("p (r h) -> p r h", h=HP)

        def G(t):
            return mid[:, (t % 2) * HP * P:(t % 2 + 1) * HP * P]

        def in_ring(sizes):
            at, views = 0, []
            for n in sizes:
                views.append(ring[:, at:at + n])
                at += n
            assert at <= 2 * P * KW
            return views

        W3, W4 = NB * MROWS, NB * 2 * BS
        modes0, modes1, hidden0, hidden1, clip0, clip1, w3, w4, bias = in_ring([2 * BANK] * 4 + [M_GROUP * BS] * 2 + [W3, W4, NB])
        modes, hidden, clip = (modes0, modes1), (hidden0, hidden1), (clip0, clip1)
        w3 = w3.rearrange("p (b r) -> p b r", r=MROWS)
        w4 = w4.rearrange("p (b r) -> p b r", r=2 * BS)
        UV, J0, J1, pair0, pair1, hid0, hid1, shrunk0, shrunk1, clip_l1, w3_l1, w4_l1, flipped0, flipped1 = in_ring(
            [NT * P, NB * MROWS, NB * MROWS] + [BANK] * 7 + [NB * MROWS, NB * HALF, C, C])
        UV = UV.rearrange("p (t n) -> p t n", n=P)
        J = [v.rearrange("p (b r) -> p b r", r=MROWS) for v in (J0, J1)]
        pair, hid, shrunk, flipped = (pair0, pair1), (hid0, hid1), (shrunk0, shrunk1), (flipped0, flipped1)
        w3_l1 = w3_l1.rearrange("p (b r) -> p b r", r=MROWS)
        w4_l1 = w4_l1.rearrange("p (b r) -> p b r", r=HALF)
        fwd_c = tables[:, 0:NT * C].rearrange("p (t c) -> p t c", c=C)
        inv_c = tables[:, NT * C:].rearrange("p (g c) -> p g c", c=C)

        Dflat = D[:, :, :].rearrange("p k c -> p (k c)")
        prep, at = {}, 0
        for name, n in (("v0", NB * MROWS), ("v1", NB * MROWS), ("v", NB * MROWS), ("q0", NB * MROWS), ("q1", NB * MROWS),
                        ("q", NB * MROWS), ("e0", NB * BS), ("e1", NB * BS), ("e", NB * BS), ("t0", NB * BS),
                        ("t1", NB * BS), ("w4", NB * HALF), ("d", NB * BS)):
            prep[name] = Dflat[:, at:at + n]
            at += n

        bank = [ctx.enter_context(nc.psum_tensor(f"bank{i}", [P, BANK], F32)) for i in range(BANKS)]

        filled = sem("filled")
        vec_emptied = sem("vec_emptied")
        act_emptied = sem("act_emptied")
        clipped = sem("clipped")
        consts_loaded = sem("consts_loaded")
        prep_loaded = sem("prep_loaded")
        prep_step = sem("prep_step")
        prep_product = sem("prep_product")
        prep_stored = sem("prep_stored")
        weights_loaded = sem("weights_loaded")
        weights_signed = sem("weights_signed")
        tables_loaded = sem("tables_loaded")
        l1_weights_loaded = sem("l1_weights_loaded")
        x_loaded = [sem(f"x_loaded{t}") for t in range(NT)]
        first_loaded = [sem(f"first_loaded{t}") for t in range(NT)]
        differed = [sem(f"differed{t}") for t in range(NT)]
        halved = sem("halved")
        mixed = [sem(f"mixed{t}") for t in range(NT)]
        stored = [sem(f"stored{t}") for t in range(NT)]
        second_stored = [sem(f"second_stored{t}") for t in range(NT)]
        pads_zeroed = sem("pads_zeroed")
        pads_written = sem("pads_written")
        flipped_loaded = [sem(f"flipped_loaded{n}") for n in range(2)]
        flipped_placed = sem("flipped_placed")
        subtracted = sem("subtracted")
        folded = sem("folded")
        v_placed = sem("v_placed")

        def rows(a):
            return a.rearrange("(h p) c -> p h c", p=P)

        class Pass:

            def __init__(self, layer, plan, fills, vec, act):
                self.layer, self.plan = layer, plan
                self.fills, self.vec, self.act = fills, vec + 1, act + 1
                self.scale_in = 1.0 if layer in (0, 1) else 1.0 / H
                self.scale_out = {0: 1.0 / TOK, 1: 2.0 / (B * TOK * C)}.get(layer, 1.0 / H)
                self.inv_h = cst("inv_h_dht" if layer == 1 else "inv_h")
                self.inv_w = cst("inv_w_dht" if layer == 1 else "inv_w")

            def bank(self, key):
                return bank[self.plan.unit[key] % BANKS]

            def fill_of(self, key):
                return self.fills + self.plan.unit[key] + 1

            def wait_filled(self, eng, key):
                eng.wait_ge(filled, self.fill_of(key))

            def wait_emptied(self, eng, key):
                if self.plan.by[key] == "vec":
                    eng.wait_ge(vec_emptied, self.vec + self.plan.emptied[key])
                else:
                    eng.wait_ge(act_emptied, self.act + self.plan.emptied[key])

            def wait_bank(self, pe, key):
                n = self.plan.unit[key] - BANKS
                if n >= 0:
                    self.wait_emptied(pe, self.plan.order[n])

            def wait_both(self, eng, stage, t, last):
                self.wait_emptied(eng, (stage, t, last - 1))
                self.wait_emptied(eng, (stage, t, last))

        def pass_l0(i):
            return Pass(0, conv, i * conv.fills, i * conv.vec, i * conv.act)

        def pass_l1(i):
            return Pass(1, dht, i * dht.fills + 2 * conv.fills, i * dht.vec + 2 * conv.vec,
                        i * dht.act + 2 * conv.act)

        def pass_l23(i, layer):
            n = layer - 2
            return Pass(layer, conv, i * (2 * conv.fills) + (2 * conv.fills + 2 * dht.fills + n * conv.fills),
                        i * (2 * conv.vec) + (2 * conv.vec + 2 * dht.vec + n * conv.vec),
                        i * (2 * conv.act) + (2 * conv.act + 2 * dht.act + n * conv.act))

        def mlp_passes_before(i, layer):
            return i if layer == 0 else i * 2 + layer

        CLIPS = 2 * STEPS

        def clips_before(i, layer):
            if layer == 0:
                return i * CLIPS
            if layer == 1:
                return i * PAIRS + 2 * CLIPS
            return i * (2 * CLIPS) + (2 * PAIRS + layer * CLIPS)

        block = ctx.enter_context(nc.Block())

        @block.sync
        def _(sp):
            sp.dma_start(const[:, :], consts).then_inc(consts_loaded, 16)

            def load_x(src, t):
                sp.dma_start(X[:, t], rows(src)[:, :, t * P:(t + 1) * P]).then_inc(x_loaded[t], 16)

            def load_weights(p, n):
                p.wait_filled(sp, ("T1", NT - 1, T1_UNITS - 1))
                sp.dma_start(w3, conv_w3[n]).then_inc(weights_loaded, 16)
                sp.dma_start(w4[0:MROWS], conv_w4[n]).then_inc(weights_loaded, 16)
                sp.dma_start(bias[0:MROWS], conv_bias[n]).then_inc(weights_loaded, 16)

            def load_first(src, p, stores):
                sp.wait_ge(filled, p.fills - TAIL)
                for t in range(NT):
                    sp.wait_ge(stored[t], 16 * stores)
                    sp.dma_start(Dflat[:, t * HP * P:(t + 1) * HP * P].rearrange("p (h c) -> p h c", c=P),
                                 rows(src)[:, :, t * P:(t + 1) * P]).then_inc(first_loaded[t], 16)

            for i in range(B):
                for t in range(NT):
                    if i > 0:
                        sp.wait_ge(stored[t], 16 * i)
                    load_x(x[i], t)
                load_weights(pass_l0(i), 0)

            load_first(after_l0[0], pass_l1(0), 1)
            sp.wait_ge(filled, 2 * conv.fills)
            sp.dma_start(tables[:, 0:NT * C], fwd_c_dram).then_inc(tables_loaded, 16)
            sp.dma_start(tables[:, NT * C:], inv_c_dram).then_inc(tables_loaded, 16)
            for t in range(NT):
                sp.wait_ge(stored[t], 16 * B)
            sp.wait_ge(prep_stored, 48)
            for i in range(B):
                p = pass_l1(i)
                if i > 0:
                    for t in range(NT):
                        sp.wait_ge(stored[t], 16 * (B + 1))
                        sp.wait_ge(second_stored[t], 16)
                        load_x(second_in, t)
                p.wait_filled(sp, ("T1", NT - 1, T1_UNITS - 1))
                sp.dma_start(w3_l1[0:MROWS].rearrange("p b r -> p (b r)"), l1_first).then_inc(l1_weights_loaded, 16)
                sp.dma_start(w4_l1[0:MROWS].rearrange("p b r -> p (b r)"), l1_second).then_inc(l1_weights_loaded, 16)
                image = after_l0[i].rearrange("(h w) c -> h w c", w=W)
                for m in range(PAIRS):
                    if m >= 2:
                        sp.wait_ge(flipped_placed, i * PAIRS + m - 1)
                    k0, nk = group(m, 2, KW)
                    for k in range(nk):
                        sp.dma_start(flipped[m % 2][k * H:(k + 1) * H], image[:, (W - k0 - k) % W]
                                     ).then_inc(flipped_loaded[m % 2], 16)

            load_first(l1_sum, pass_l23(0, 2), B + 1)
            for i in range(B):
                if i > 0:
                    for t in range(NT):
                        sp.wait_ge(stored[t], 16 * (B + 2))
                        sp.wait_ge(second_stored[t], 32)
                        load_x(second_in, t)
                load_weights(pass_l23(i, 2), 1)
                load_weights(pass_l23(i, 3), 2)

        @block.gpsimd
        def _(pool):
            for n in range(2):
                pool.dma_start(prep[f"v{n}"][0:MROWS], l1_w3[n]).then_inc(prep_loaded, 16)
                pool.dma_start(prep[f"q{n}"][0:BS], l1_q[n]).then_inc(prep_loaded, 16)
                pool.dma_start(prep[f"e{n}"][0:BS], l1_e[n]).then_inc(prep_loaded, 16)
                pool.dma_start(prep[f"t{n}"][0:MROWS], l1_t[n]).then_inc(prep_loaded, 16)
            pool.dma_start(prep["d"][0:BS], l1_e[2]).then_inc(prep_loaded, 16)
            pool.wait_ge(prep_step, PREP_STEPS)
            pool.dma_start(l1_first, prep["v"][0:MROWS]).then_inc(prep_stored, 16)
            pool.dma_start(l1_second, prep["w4"][0:MROWS]).then_inc(prep_stored, 16)
            pool.wait_ge(prep_stored, 32)
            pool.dma_start(l1_first[ONE:ONE + 1], l1_w3_bias).then_inc(prep_stored, 16)

            def store(p, dst):
                for t in range(NT):
                    p.wait_emptied(pool, ("S6", t, INV_UNITS - 1))
                    pool.dma_start(rows(dst)[:, :, t * P:(t + 1) * P], X[:, t]).then_inc(stored[t], 16)

            def store_second(n):
                for t in range(NT):
                    pool.wait_ge(differed[t], n)
                    if n == 2:
                        pool.wait_ge(halved, t + 1)
                    pool.dma_start(rows(second_in)[:, :, t * P:(t + 1) * P],
                                   Dflat[:, t * HP * P:(t + 1) * HP * P].rearrange("p (h c) -> p h c", c=P)
                                   ).then_inc(second_stored[t], 16)

            def zero_pads(p):
                if p.fills > 0:
                    pool.wait_ge(filled, p.fills)
                nc.gpsimd.memset(Bpad[:, :, :, BS:], 0.0).then_inc(pads_zeroed, 1)

            for i in range(B):
                zero_pads(pass_l0(i))
                store(pass_l0(i), after_l0[i])
            store_second(1)
            for i in range(B):
                p = pass_l1(i)
                for m in range(PAIRS):
                    k0, nk = group(m, 2, KW)
                    columns = [sum(group(n, 2, KW)[1] for n in range(m % 2, end, 2)) for end in (m + 1, PAIRS)]
                    pool.wait_ge(flipped_loaded[m % 2], 16 * (i * columns[1] + columns[0]))
                    if m >= 2:
                        p.wait_filled(pool, ("TJ", m - 2, 1))
                    n = nk * H
                    nc.gpsimd.tensor_copy(
                        J[m % 2][0:n, :, HALF:MROWS].rearrange("p b (t c) -> p b t c", t=NT),
                        flipped[m % 2][0:n].rearrange("p (t b c) -> p b t c", t=NT, b=NB)).then_inc(flipped_placed, 1)
                if i == 0:
                    store(p, l1_sum)
            store_second(2)
            for i in range(B):
                zero_pads(pass_l23(i, 2))
                zero_pads(pass_l23(i, 3))
                store(pass_l23(i, 3), out[i])
            for t in range(NT):
                pool.wait_ge(stored[t], 16 * (2 * B + 1))
                pool.wait_ge(second_stored[t], 32)

        @block.tensor
        def _(pe):
            def forward(p, x_ready):
                pe.wait_ge(vec_emptied, p.vec)
                pe.wait_ge(act_emptied, p.act)

                def s1(t):
                    x_ready(t)
                    for g in range(S1_UNITS):
                        key = ("S1", t, g)
                        p.wait_bank(pe, key)
                        h0, nh = group(g, S1_GROUP, HP)
                        for k in range(nh):
                            n = 4 * KW
                            mm = nc.tensor.matmul(p.bank(key)[:, k * n:(k + 1) * n], X[:, t, h0 + k], dft_w,
                                                  start=True, stop=True)
                        mm.then_inc(filled, 1)

                def t1(t):
                    p.wait_both(pe, "S1", t, S1_UNITS - 1)
                    for g in range(T1_UNITS):
                        key = ("T1", t, g)
                        p.wait_bank(pe, key)
                        k0, nk = group(g, T_GROUP, KW)
                        for k in range(nk):
                            mm = nc.tensor.transpose(p.bank(key)[:, k * P:(k + 1) * P], A(t)[:, :, k0 + k], identity)
                        mm.then_inc(filled, 1)

                s1(0)
                s1(1)
                t1(0)
                s1(2)
                t1(1)
                t1(2)
                p.wait_both(pe, "T1", NT - 1, T1_UNITS - 1)

            def inverse(p):
                def s5(t):
                    for u in range(INV_UNITS):
                        key = ("S5", t, u)
                        p.wait_bank(pe, key)
                        kws = [0, KW - 1, 1, 2, 3] if u == 0 else range(4 * u, 4 * u + 4)
                        at = 0
                        for k in kws:
                            rhs = p.inv_h[:, 2 * H:3 * H] if k in (0, KW - 1) else p.inv_h[:, 0:2 * H]
                            n = rhs.shape[1]
                            mm = nc.tensor.matmul(p.bank(key)[:, at:at + n], D[:, k, t * P:(t + 1) * P], rhs,
                                                  start=True, stop=True)
                            at += n
                        mm.then_inc(filled, 1)

                def t2(t):
                    p.wait_both(pe, "S5", t, INV_UNITS - 1)
                    for u in range(INV_UNITS):
                        key = ("T2", t, u)
                        p.wait_bank(pe, key)
                        for k in range(T_GROUP):
                            mm = nc.tensor.transpose(p.bank(key)[:, k * P:(k + 1) * P], E(t)[:, :, u * T_GROUP + k],
                                                     identity)
                        mm.then_inc(filled, 1)

                def s6(t):
                    p.wait_both(pe, "T2", t, INV_UNITS - 1)
                    for u in range(INV_UNITS):
                        key = ("S6", t, u)
                        p.wait_bank(pe, key)
                        nc.tensor.matmul(p.bank(key)[:, :], p.inv_w, G(t)[:, u * BANK:(u + 1) * BANK],
                                         start=True, stop=True).then_inc(filled, 1)

                s5(0)
                s5(1)
                t2(0)
                s5(2)
                t2(1)
                s6(0)
                t2(2)
                s6(1)
                s6(2)

            def mlp(p, i):
                def s2(n):
                    a, (k0, nk) = n // M_GROUPS, group(n % M_GROUPS, M_GROUP, KW)
                    for u in range(s2_units(n)):
                        key = ("S2", n, u)
                        p.wait_bank(pe, key)
                        at, cols = group(u, T_GROUP, nk)
                        for k in range(cols):
                            mm = nc.tensor.matmul(p.bank(key)[:, k * P:(k + 1) * P], Bpair[:, k0 + at + k, a], dft_h,
                                                  start=True, stop=True)
                        mm.then_inc(filled, 1)

                def s3(n):
                    a, (_, nk) = n // M_GROUPS, group(n % M_GROUPS, M_GROUP, KW)
                    p.wait_emptied(pe, ("S2", n, s2_units(n) - 1))
                    for b in range(2):
                        key = ("S3", n, b)
                        p.wait_bank(pe, key)
                        nc.tensor.matmul(p.bank(key)[0:MROWS, 0:nk * H], w3[:, 2 * a + b],
                                         modes[n % 2][:, b * BANK:b * BANK + nk * H],
                                         start=True, stop=True).then_inc(filled, 1)

                def s4(n):
                    a, (_, nk) = n // M_GROUPS, group(n % M_GROUPS, M_GROUP, KW)
                    for b in range(2):
                        key = ("S4", n, b)
                        p.wait_bank(pe, key)
                        p.wait_emptied(pe, ("S3", n, b))
                        for k in range(-(-nk // 2)):
                            tok = min(P, nk * H)
                            mm = nc.tensor.matmul(p.bank(key)[0:tok, k * 2 * BS:(k + 1) * 2 * BS],
                                                  hidden[n % 2][0:MROWS, b * BANK + k * P:b * BANK + k * P + tok],
                                                  w4[0:MROWS, 2 * a + b], start=True, stop=True)
                        mm.then_inc(filled, 1)

                passes = mlp_passes_before(i, p.layer)
                pe.wait_ge(pads_zeroed, passes + 1)
                for n in range(STEPS + 2):
                    if n < STEPS:
                        s2(n)
                    if n == 1:
                        pe.wait_ge(weights_signed, passes * 2 + 2)
                    if 0 <= n - 1 < STEPS:
                        s3(n - 1)
                    if 0 <= n - 2 < STEPS:
                        s4(n - 2)
                p.wait_emptied(pe, ("S4", STEPS - 1, 1))

            def hartley(p, i):
                def f2(m):
                    k0, nk = group(m, 2, KW)
                    pe.wait_ge(folded, i * PAIRS + (m + 1))
                    for k in range(nk):
                        key = ("F2", m, k)
                        p.wait_bank(pe, key)
                        for t in range(NT):
                            mm = nc.tensor.matmul(p.bank(key)[:, t * P:(t + 1) * P], Bm[:, k0 + k, t * P:(t + 1) * P],
                                                  dft_h_uv, start=True, stop=True)
                        mm.then_inc(filled, 1)

                def cf(m):
                    key, nk = ("CF", m), group(m, 2, KW)[1]
                    p.wait_bank(pe, key)
                    p.wait_emptied(pe, ("F2", m, nk - 1))
                    for t in range(NT):
                        mm = nc.tensor.matmul(p.bank(key)[0:nk * H, 0:C], UV[:, t, 0:nk * H], fwd_c[:, t],
                                              start=t == 0, stop=t == NT - 1)
                    mm.then_inc(filled, 1)

                def tj(m):
                    p.wait_emptied(pe, ("CF", m))
                    pe.wait_ge(flipped_placed, i * PAIRS + (m + 1))
                    for half in range(2):
                        key = ("TJ", m, half)
                        p.wait_bank(pe, key)
                        for b in range(4):
                            mm = nc.tensor.transpose(p.bank(key)[0:MROWS, b * P:(b + 1) * P], J[m % 2][:, half * 4 + b],
                                                     identity)
                        mm.then_inc(filled, 1)

                def h1(m):
                    nk = group(m, 2, KW)[1]
                    for half in range(2):
                        key = ("H1", m, half)
                        p.wait_bank(pe, key)
                        p.wait_emptied(pe, ("TJ", m, half))
                        for b in range(4):
                            mm = nc.tensor.matmul(p.bank(key)[0:MROWS, b * P:b * P + nk * H],
                                                  w3_l1[0:MROWS, half * 4 + b], pair[half][0:MROWS, b * P:b * P + nk * H],
                                                  start=True, stop=True)
                        mm.then_inc(filled, 1)

                def h2(m):
                    key, nk = ("H2", m), group(m, 2, KW)[1]
                    p.wait_bank(pe, key)
                    p.wait_emptied(pe, ("H1", m, 1))
                    for b in range(NB):
                        row, g = b % 2 * HALF, b // 2
                        mm = nc.tensor.matmul(p.bank(key)[row:row + HALF, g * P:g * P + nk * H], w4_l1[0:MROWS, b],
                                              hid[b // 4][0:MROWS, b % 4 * P:b % 4 * P + nk * H],
                                              start=True, stop=True)
                    mm.then_inc(filled, 1)

                def ci(m):
                    p.wait_emptied(pe, ("H2", m))
                    n = group(m, 2, KW)[1] * H
                    for part, cols in (("even", slice(0, EVEN)), ("odd", slice(EVEN, C))):
                        key = ("CI", m, part)
                        p.wait_bank(pe, key)
                        for g in range(NB // 2):
                            mm = nc.tensor.matmul(p.bank(key)[0:n, 0:cols.stop - cols.start],
                                                  shrunk[m % 2][:, g * P:g * P + n], inv_c[:, g, cols],
                                                  start=g == 0, stop=g == NB // 2 - 1)
                        mm.then_inc(filled, 1)

                f2(0)
                pe.wait_ge(tables_loaded, 32)
                cf(0)
                pe.wait_ge(pads_written, i * 2 + 2)
                pe.wait_ge(l1_weights_loaded, i * 32 + 32)
                for m in range(PAIRS):
                    tj(m)
                    if m + 1 < PAIRS:
                        f2(m + 1)
                    h1(m)
                    if m + 1 < PAIRS:
                        cf(m + 1)
                    h2(m)
                    if m > 0:
                        ci(m - 1)
                ci(PAIRS - 1)
                p.wait_emptied(pe, ("CI", PAIRS - 1, "even"))
                p.wait_emptied(pe, ("CI", PAIRS - 1, "odd"))

            pe.wait_ge(prep_step, PREP_OPERANDS)
            for b in range(NB):
                mm = nc.tensor.matmul(bank[BANKS - 1][0:MROWS, b * BS:(b + 1) * BS],
                                      prep["q"][0:BS, b * MROWS:(b + 1) * MROWS], prep["e"][0:BS, b * BS:(b + 1) * BS],
                                      start=True, stop=True)
            mm.then_inc(prep_product, 1)
            pe.wait_ge(consts_loaded, 16)
            pe.wait_ge(prep_step, PREP_STEPS)

            with pe.Fori(0, B) as i:
                p = pass_l0(i)
                forward(p, lambda t: pe.wait_ge(x_loaded[t], i * 16 + 16))
                mlp(p, i)
                inverse(p)

            def joined(t, n, loads):
                pe.wait_ge(mixed[t], n)
                pe.wait_ge(x_loaded[t], loads)

            with pe.Fori(0, B) as i:
                p = pass_l1(i)
                forward(p, lambda t: joined(t, 1, i * 16 + 16 * B))
                hartley(p, i)
                inverse(p)
            with pe.Fori(0, B) as i:
                for layer in (2, 3):
                    p = pass_l23(i, layer)
                    forward(p, lambda t: joined(t, 2, i * 16 + 16 * (B + 1)))
                    mlp(p, i)
                    inverse(p)

        def empty_forward(p, eng, me, copy, emptied):
            for key in p.plan.order:
                if key[0] not in ("S1", "T1") or p.plan.by[key] != me:
                    continue
                stage, t, g = key
                p.wait_filled(eng, key)
                if stage == "S1":
                    h0, nh = group(g, S1_GROUP, HP)
                    dst = A(t)[:, :, :].rearrange("p (a h) k -> p h a k", h=HP)[:, h0:h0 + nh]
                    src = p.bank(key)[:, 0:nh * 4 * KW].rearrange("p (h a k) -> p h a k", a=4, k=KW)
                else:
                    k0, nk = group(g, T_GROUP, KW)
                    if p.layer == 1:
                        dst = Bm[:, k0:k0 + nk, t * P:(t + 1) * P]
                        src = p.bank(key)[:, 0:nk * P].rearrange("p (k c) -> p k c", c=P)
                    else:
                        dst = Bpad[:, k0:k0 + nk, :, t * TB:(t + 1) * TB]
                        src = p.bank(key)[:, 0:nk * P].rearrange("p (k b c) -> p k b c", b=NB, c=TB)
                copy(dst, src).then_inc(emptied, 1)

        def empty_inverse(p, eng, me, copy, emptied):
            for key in p.plan.order:
                if key[0] not in ("S5", "T2", "S6") or p.plan.by[key] != me:
                    continue
                stage, t, u = key
                p.wait_filled(eng, key)
                if stage == "S5":
                    dst = E(t).rearrange("p (j q) h -> p q j h", j=2)[:, 8 * u:8 * u + 8]
                    copy(dst, p.bank(key)[:, :].rearrange("p (q j h) -> p q j h", j=2, h=HP)).then_inc(emptied, 1)
                elif stage == "T2":
                    copy(G(t)[:, u * BANK:(u + 1) * BANK], p.bank(key)[:, :]).then_inc(emptied, 1)
                else:
                    rows4 = X[:, t, 4 * u:4 * u + 4].rearrange("p h c -> p (h c)")
                    nc.vector.scalar_tensor_tensor(out=rows4, in0=p.bank(key)[:, :], scalar=p.scale_out, in1=rows4,
                                                   op0=ALU.mult, op1=ALU.add).then_inc(emptied, 1)

        @block.scalar
        def _(act):
            def copy(dst, src):
                return nc.scalar.activation(dst, src, ACT.Copy)

            def mlp(p, i):
                for n in range(STEPS + 1):
                    if n < STEPS:
                        nk = group(n % M_GROUPS, M_GROUP, KW)[1]
                        for u in range(s2_units(n)):
                            key = ("S2", n, u)
                            at, cols = group(u, T_GROUP, nk)
                            p.wait_filled(act, key)
                            for b in range(2):
                                src = p.bank(key)[b * HALF:(b + 1) * HALF, 0:cols * P].rearrange(
                                    "p (k a h) -> p k a h", a=2, h=H)
                                for ri in range(2):
                                    lo = b * BANK + at * H
                                    dst = modes[n % 2][ri * HALF:(ri + 1) * HALF, lo:lo + cols * H]
                                    moved = nc.scalar.activation(dst.rearrange("p (k h) -> p k h", h=H),
                                                                 src[:, :, ri], ACT.Copy, scale=p.scale_in)
                            moved.then_inc(act_emptied, 1)
                    if n == 0:
                        act.wait_ge(weights_loaded, mlp_passes_before(i, p.layer) * 48 + 48)
                    if n > 0:
                        nk, a = group((n - 1) % M_GROUPS, M_GROUP, KW)[1], (n - 1) // M_GROUPS
                        for b in range(2):
                            key, lo, blk = ("S3", n - 1, b), b * BANK, 2 * a + b
                            p.wait_filled(act, key)
                            nc.scalar.activation(hidden[(n - 1) % 2][0:MROWS, lo:lo + nk * H],
                                                 p.bank(key)[0:MROWS, 0:nk * H], ACT.Relu,
                                                 bias=bias[0:MROWS, blk:blk + 1]).then_inc(act_emptied, 1)

            def hartley(p, i):
                def f2(m):
                    for k in range(group(m, 2, KW)[1]):
                        key = ("F2", m, k)
                        p.wait_filled(act, key)
                        cols = slice(k * H, (k + 1) * H)
                        src = p.bank(key)[:, 0:NT * P].rearrange("p (t a n) -> p t a n", a=2, n=H)
                        copy(UV[HALF:P, 0, cols], src[HALF:P, 0, 1]).then_inc(v_placed, 1)
                        copy(UV[0:HALF, 0, cols], src[0:HALF, 0, 0])
                        copy(UV[:, 1, cols], src[:, 1, 0])
                        copy(UV[:, 2, cols], src[:, 2, 1])
                        act.wait_ge(v_placed, i * KW + (2 * m + k + 1))
                        copy(UV[HALF:MIDDLE, 0, cols], src[HALF:MIDDLE, 0, 0]).then_inc(act_emptied, 1)

                def ci(m):
                    key = ("CI", m, "even")
                    p.wait_filled(act, key)
                    k0, nk = group(m, 2, KW)
                    for k in range(nk):
                        src, dst = p.bank(key)[k * H:(k + 1) * H, 0:EVEN], D[0:H, k0 + k]
                        copy(dst[:, 0:MIDDLE], src[:, 0:MIDDLE])
                        copy(dst[:, P:2 * P], src[:, MIDDLE:])
                        copy(dst[:, P - 1:P - MIDDLE + 1:-1], src[:, 1:MIDDLE - 1])
                        last = copy(dst[:, C - 1:2 * P - 1:-1], src[:, MIDDLE:])
                    last.then_inc(act_emptied, 1)

                f2(0)
                for m in range(PAIRS):
                    n = group(m, 2, KW)[1] * H
                    for half in range(2):
                        key = ("TJ", m, half)
                        p.wait_filled(act, key)
                        copy(pair[half][0:MROWS].rearrange("p (b n) -> p b n", n=P)[:, :, 0:n],
                             p.bank(key)[0:MROWS].rearrange("p (b n) -> p b n", n=P)[:, :, 0:n]).then_inc(act_emptied, 1)
                    if m + 1 < PAIRS:
                        f2(m + 1)
                    for half in range(2):
                        key = ("H1", m, half)
                        p.wait_filled(act, key)
                        nc.scalar.activation(hid[half][0:MROWS].rearrange("p (b n) -> p b n", n=P)[:, :, 0:n],
                                             p.bank(key)[0:MROWS].rearrange("p (b n) -> p b n", n=P)[:, :, 0:n],
                                             ACT.Relu).then_inc(act_emptied, 1)
                    if m > 0:
                        ci(m - 1)
                ci(PAIRS - 1)

            act.wait_ge(vec_emptied, 1)
            nc.scalar.activation(warm[:, 1:2], warm[:, 0:1], ACT.Relu).then_inc(act_emptied, 1)
            with act.Fori(0, B) as i:
                p = pass_l0(i)
                empty_forward(p, act, "act", copy, act_emptied)
                mlp(p, i)
                empty_inverse(p, act, "act", copy, act_emptied)
            with act.Fori(0, B) as i:
                p = pass_l1(i)
                empty_forward(p, act, "act", copy, act_emptied)
                hartley(p, i)
                empty_inverse(p, act, "act", copy, act_emptied)
            with act.Fori(0, B) as i:
                for layer in (2, 3):
                    p = pass_l23(i, layer)
                    empty_forward(p, act, "act", copy, act_emptied)
                    mlp(p, i)
                    empty_inverse(p, act, "act", copy, act_emptied)

        @block.vector
        def _(vec):
            def copy(dst, src):
                return nc.vector.tensor_copy(dst, src)

            def clip_to(p, key, held, src, clips, done):
                p.wait_filled(vec, key)
                if done is not None:
                    vec.wait_ge(vec_emptied, p.vec + done)
                nc.vector.tensor_scalar(held, src, -LAMBDA, LAMBDA, ALU.max, ALU.min).then_inc(clipped, 1)
                vec.wait_ge(clipped, clips)

            def set_signs(p, i):
                vec.wait_ge(weights_loaded, mlp_passes_before(i, p.layer) * 48 + 48)
                for w, end in ((w3, P), (w4, MROWS)):
                    nc.vector.tensor_scalar(w[HALF:end, :, 0:BS], w[HALF:end, :, 0:BS], -1.0, None,
                                            ALU.mult).then_inc(weights_signed, 1)

            def mlp(p, i):
                set_signs(p, i)
                clips = clips_before(i, p.layer)
                Dtiles = D[:, :, :].rearrange("p k (t b c) -> p k t b c", t=NT, b=NB)
                for n in range(STEPS):
                    a, (k0, nk) = n // M_GROUPS, group(n % M_GROUPS, M_GROUP, KW)
                    pairs, parts = -(-nk // 2), min(2, nk)
                    for b in range(2):
                        key = ("S4", n, b)
                        cols = pairs * 2 * BS
                        src, held = p.bank(key)[0:parts * H, 0:cols], clip[b][0:parts * H, 0:cols]
                        clip_to(p, key, held, src, clips + (2 * n + b + 1),
                                p.plan.emptied[("S4", n - 1, b)] if n else None)
                        src, held = (v.rearrange("p (k a t c) -> p k a t c", a=2, t=NT, c=TB) for v in (src, held))
                        for part in range(parts):
                            half = slice(part * H, (part + 1) * H)
                            for ri in range(2):
                                dst = Dtiles[ri * H:(ri + 1) * H, k0 + part:k0 + nk:2, :, 2 * a + b]
                                moved = nc.vector.tensor_tensor(dst, src[half, :, ri], held[half, :, ri], ALU.subtract)
                        moved.then_inc(vec_emptied, 1)

            def hartley(p, i):
                clips = clips_before(i, 1)
                p.wait_filled(vec, ("T1", NT - 1, T1_UNITS - 1))
                both = ring[:, NT * P:NT * P + 2 * NB * MROWS].rearrange("p (b r) -> p b r", r=MROWS)
                nc.vector.memset(both[:, :, ONE:ONE + 1], 1.0).then_inc(pads_written, 1)
                nc.vector.memset(both[:, :, ONE + 1:HALF], 0.0).then_inc(pads_written, 1)

                def cf(m):
                    key, n = ("CF", m), group(m, 2, KW)[1] * H
                    p.wait_filled(vec, key)
                    copy(J[m % 2][0:n, :, 0:BS],
                         p.bank(key)[0:n, 0:C].rearrange("p (b c) -> p b c", c=BS)).then_inc(vec_emptied, 1)

                def ci(m):
                    key = ("CI", m, "odd")
                    p.wait_filled(vec, key)
                    k0, nk = group(m, 2, KW)
                    for k in range(nk):
                        src, dst = p.bank(key)[k * H:(k + 1) * H, 0:C - EVEN], D[H:P, k0 + k]
                        copy(dst[:, MIDDLE:P], src[:, 0:P - MIDDLE])
                        copy(dst[:, 2 * P:], src[:, P - MIDDLE:])
                        nc.vector.tensor_scalar(dst[:, P - MIDDLE:0:-1], src[:, 0:P - MIDDLE], -1.0, None, ALU.mult)
                        last = nc.vector.tensor_scalar(dst[:, 2 * P - 1:P - 1:-1], src[:, P - MIDDLE:], -1.0, None,
                                                       ALU.mult)
                    last.then_inc(vec_emptied, 1)

                def fold(m):
                    k0, nk = group(m, 2, KW)
                    b = Bm[:, k0:k0 + nk]
                    ranges = ((b[:, :, 1:P - MIDDLE + 1], b[:, :, P - 1:MIDDLE - 1:-1]),
                              (b[:, :, P:2 * P], b[:, :, C - 1:2 * P - 1:-1]))
                    for low, high in ranges:
                        nc.vector.tensor_tensor(high, low, high, ALU.subtract).then_inc(subtracted, 1)
                    vec.wait_ge(subtracted, i * (2 * PAIRS) + (2 * m + 2))
                    for low, high in ranges:
                        last = nc.vector.scalar_tensor_tensor(out=low, in0=low, scalar=2.0, in1=high,
                                                              op0=ALU.mult, op1=ALU.subtract)
                    last.then_inc(folded, 1)

                p.wait_both(vec, "T1", NT - 1, T1_UNITS - 1)
                fold(0)
                fold(1)
                for c in (0, MIDDLE - 1):
                    nc.vector.memset(D[H:P, :, c:c + 1], 0.0)
                cf(0)
                for m in range(PAIRS):
                    if m + 1 < PAIRS:
                        cf(m + 1)
                    if m + 2 < PAIRS:
                        fold(m + 2)
                    key, n = ("H2", m), group(m, 2, KW)[1] * H
                    src, held, dst = (v.rearrange("p (g n) -> p g n", n=P)[:, :, 0:n]
                                      for v in (p.bank(key)[:, :], clip_l1, shrunk[m % 2]))
                    clip_to(p, key, held, src, clips + (m + 1), p.plan.emptied[("H2", m - 1)] if m else None)
                    nc.vector.tensor_tensor(dst, src, held, ALU.subtract).then_inc(vec_emptied, 1)
                    if m > 0:
                        ci(m - 1)
                ci(PAIRS - 1)

            def mix(n, last, factor):
                for t in range(NT):
                    tile = X[:, t].rearrange("p h c -> p (h c)")
                    other = Dflat[:, t * HP * P:(t + 1) * HP * P]
                    last.wait_emptied(vec, ("S6", t, INV_UNITS - 1))
                    vec.wait_ge(first_loaded[t], 16 * n)
                    nc.vector.tensor_tensor(other, other, tile, ALU.subtract).then_inc(differed[t], 1)
                    vec.wait_ge(differed[t], n)
                    if n == 1:
                        vec.wait_ge(stored[t], 16 * B)
                    else:
                        nc.vector.tensor_scalar(other, other, 0.5, None, ALU.mult).then_inc(halved, 1)
                        vec.wait_ge(halved, t + 1)
                    nc.vector.scalar_tensor_tensor(out=tile, in0=tile, scalar=factor, in1=other,
                                                   op0=ALU.mult, op1=ALU.add).then_inc(mixed[t], 1)

            nc.vector.memset(warm[:, 0:1], 0.0).then_inc(vec_emptied, 1)

            steps = 0

            def step(ins):
                nonlocal steps
                steps += 1
                ins.then_inc(prep_step, 1)

            def after_steps():
                vec.wait_ge(prep_step, steps)

            def blocks(name, r):
                return prep[name].rearrange("p (b r) -> p b r", r=r)

            vec.wait_ge(prep_loaded, 9 * 16)
            q0, q1, q = (blocks(n, MROWS) for n in ("q0", "q1", "q"))
            step(nc.vector.tensor_tensor(q[0:BS, :, 0:HALF], q0[0:BS, :, 0:HALF], q1[0:BS, :, 0:HALF], ALU.add))
            step(nc.vector.tensor_tensor(q[0:BS, :, HALF:], q0[0:BS, :, HALF:], q1[0:BS, :, HALF:], ALU.subtract))
            step(nc.vector.tensor_tensor(prep["e"][0:BS], prep["e0"][0:BS], prep["e1"][0:BS], ALU.subtract))
            after_steps()
            step(nc.vector.tensor_scalar(q[0:BS, :, 0:BS], q[0:BS, :, 0:BS], 0.5, None, ALU.mult))
            step(nc.vector.tensor_scalar(q[0:BS, :, HALF:], q[0:BS, :, HALF:], 0.5, None, ALU.mult))
            step(nc.vector.scalar_tensor_tensor(out=prep["e"][0:BS], in0=prep["e"][0:BS], scalar=0.5,
                                                in1=prep["d"][0:BS], op0=ALU.mult, op1=ALU.add))
            v0, v1, v = (blocks(n, MROWS) for n in ("v0", "v1", "v"))
            for rows_, first in ((slice(0, HALF), ALU.add), (slice(HALF, MROWS), ALU.subtract)):
                second = ALU.subtract if first == ALU.add else ALU.add
                step(nc.vector.tensor_tensor(v[rows_, :, 0:HALF], v0[rows_, :, 0:HALF], v1[rows_, :, 0:HALF], first))
                step(nc.vector.tensor_tensor(v[rows_, :, HALF:], v0[rows_, :, HALF:], v1[rows_, :, HALF:], second))
            after_steps()
            assert steps == PREP_OPERANDS
            step(nc.vector.tensor_scalar(prep["v"][0:MROWS], prep["v"][0:MROWS], 0.5, None, ALU.mult))
            t0, t1 = prep["t0"], prep["t1"]
            step(nc.vector.tensor_tensor(t0[0:MROWS], t0[0:MROWS], t1[0:MROWS], ALU.add))
            step(nc.vector.memset(prep["w4"][0:MROWS], 0.0))
            after_steps()
            step(nc.vector.tensor_scalar(t0[HALF:MROWS], t0[HALF:MROWS], 0.5, None, ALU.mult))
            after_steps()
            vec.wait_ge(prep_product, 1)
            step(nc.vector.tensor_tensor(
                blocks("w4", HALF)[0:MROWS, :, 0:BS],
                bank[BANKS - 1][0:MROWS, 0:NB * BS].rearrange("p (b c) -> p b c", c=BS),
                blocks("t0", BS)[0:MROWS], ALU.add))
            assert steps == PREP_STEPS
            vec.wait_ge(prep_stored, 48)

            with vec.Fori(0, B) as i:
                p = pass_l0(i)
                empty_forward(p, vec, "vec", copy, vec_emptied)
                mlp(p, i)
                empty_inverse(p, vec, "vec", copy, vec_emptied)
            mix(1, pass_l0(1), 2.0)
            with vec.Fori(0, B) as i:
                p = pass_l1(i)
                empty_forward(p, vec, "vec", copy, vec_emptied)
                for t in range(NT):
                    vec.wait_ge(second_stored[t], 16)
                hartley(p, i)
                empty_inverse(p, vec, "vec", copy, vec_emptied)
            mix(2, pass_l1(1), 1.0)
            with vec.Fori(0, B) as i:
                for layer in (2, 3):
                    p = pass_l23(i, layer)
                    empty_forward(p, vec, "vec", copy, vec_emptied)
                    for t in range(NT):
                        vec.wait_ge(second_stored[t], 32)
                    mlp(p, i)
                    empty_inverse(p, vec, "vec", copy, vec_emptied)


def lay_out_conv(w1, b1, w2, b2):
    w3 = np.zeros((P, NB, MROWS), np.float32)
    w4 = np.zeros((MROWS, NB, 2 * BS), np.float32)
    bias = np.zeros((MROWS, NB), np.float32)
    s = slots()
    for b in range(NB):
        for rows, first, second in ((0, 0, 1), (HALF, 1, 0)):
            w3[rows:rows + BS, b, 0:BS] = w1[first, b][s]
            w3[rows:rows + BS, b, HALF:] = w1[second, b][s]
            w4[rows:rows + BS, b, 0:BS] = w2[first, b][:, s]
            w4[rows:rows + BS, b, BS:] = w2[second, b][:, s]
            bias[rows:rows + BS, b] = b1[first, b]
        w4[ONE, b, 0:BS], w4[ONE, b, BS:] = b2[0, b][s], b2[1, b][s]
    bias[ONE] = 1.0
    return w3, w4, bias


def lay_out_hartley(w1, b1, w2, b2):
    first = np.zeros((2, MROWS, NB, MROWS), np.float32)
    first_bias = np.zeros((1, NB, MROWS), np.float32)
    q = np.zeros((2, BS, NB, MROWS), np.float32)
    e = np.zeros((3, BS, NB, BS), np.float32)
    t = np.zeros((2, MROWS, NB, BS), np.float32)
    s = slots()
    for b in range(NB):
        for n in range(2):
            for r in (0, HALF):
                for c in (0, HALF):
                    first[n, r:r + BS, b, c:c + BS] = w1[n, b][s]
                q[n, :, b, r:r + BS] = w2[n, b].T
            e[n, :, b] = w2[n, b][:, s]
            t[n, HALF:, b] = w2[n, b][:, s]
        first_bias[0, b, 0:BS], first_bias[0, b, HALF:] = b1[0, b], b1[1, b]
        first_bias[0, b, ONE] = 1.0
        q[0, :, b, ONE] = b2[0, b]
        t[0, ONE, b] = b2[1, b][s]
        e[2, :, b] = np.eye(BS)[:, s]
    return first, first_bias, q, e, t


def kernel(x, **weights):
    import concourse.bacc as bacc
    from concourse import mybir
    from concourse.bass_utils import run_bass_kernel_spmd

    w = {n: np.asarray(a) for n, a in weights.items()}
    for n in ("L2_conv_w1", "L2_conv_b1", "L2_conv_w2", "L2_conv_b2"):
        w[n] = np.moveaxis(w[n], -1, 0)
    layers = {n: [w[f"L{n}_conv_{k}"] for k in ("w1", "b1", "w2", "b2")] for n in range(4)}
    laid = [lay_out_conv(*layers[n]) for n in (0, 2, 3)]
    first, first_bias, q, e, t = lay_out_hartley(*layers[1])
    parts, fwd_c, inv_c = constants()
    const_at, at = {}, 0
    for name, a in parts.items():
        const_at[name] = (at, a.shape[1])
        at += a.shape[1]
    arrays = {
        "x": np.asarray(x).reshape(B, TOK, P, NT).swapaxes(2, 3).reshape(B, TOK, C),
        "consts": np.concatenate(list(parts.values()), 1),
        "fwd_c": fwd_c,
        "inv_c": inv_c,
        "conv_w3": np.stack([a[0] for a in laid]),
        "conv_w4": np.stack([a[1] for a in laid]),
        "conv_bias": np.stack([a[2] for a in laid]),
        "l1_w3": first.reshape(2, MROWS, -1),
        "l1_w3_bias": first_bias.reshape(1, -1),
        "l1_q": q.reshape(2, BS, -1),
        "l1_e": e.reshape(3, BS, -1),
        "l1_t": t.reshape(2, MROWS, -1),
    }
    arrays = {n: np.ascontiguousarray(a) for n, a in arrays.items()}
    nc = bacc.Bacc("TRN2", target_bir_lowering=False, num_devices=1)
    ins = [nc.dram_tensor(n, a.shape, mybir.dt.float32, kind="ExternalInput").ap() for n, a in arrays.items()]
    out = nc.dram_tensor("out", (B, TOK, C), mybir.dt.float32, kind="ExternalOutput").ap()
    build(nc, *ins, out, const_at)
    r = run_bass_kernel_spmd(nc, [arrays], core_ids=[0])
    return r.results[0]["out"].reshape(B, TOK, NT, P).swapaxes(2, 3).reshape(B, H, W, C)
```

```python
import numpy as np

B, H, W, C = 2, 64, 64, 384
NB = 8
BS = C // NB
P = 128
NT = C // P
HP = H // 2
KW = W // 2 + 1
Q = 64
TOK = H * W
BANK = 512
BANKS = 8
ONE = BS
HALF = 64
MROWS = HALF + BS
LAMBDA = 0.01

S1_GROUP = 3
S1_UNITS = -(-HP // S1_GROUP)
T_GROUP = BANK // P
T1_UNITS = -(-KW // T_GROUP)
M_GROUP = BANK // H
M_SIZES = [M_GROUP, M_GROUP, 6, 6, 5]
STEPS = NB // 2 * len(M_SIZES)
TB = BS // NT
INV_UNITS = Q * H // BANK
S5_ORDER = [*range(1, INV_UNITS), 0]
TILE_PARTS = 4
PAIRS = -(-KW // 2)
EVEN = C // 2 + 1
MIDDLE = P // 2 + 1
PREP_OPERANDS, PREP_STEPS = 6, 10
VECTOR_DIFFS = 2
TAIL = 3 * INV_UNITS


def group(n, size, total):
    return n * size, min(size, total - n * size)


def forward_order():
    s1 = [[("S1", t, g) for g in range(S1_UNITS)] for t in range(NT)]
    t1 = [[("T1", t, g) for g in range(T1_UNITS)] for t in range(NT)]
    return s1[0] + s1[1] + t1[0] + s1[2] + t1[1] + t1[2]


def inverse_order():
    s5, t2, s6 = ([[(s, t, u) for u in units] for t in range(NT)]
                  for s, units in (("S5", S5_ORDER), ("T2", range(INV_UNITS)), ("S6", range(INV_UNITS))))
    return s5[0] + s5[1] + t2[0] + t2[1] + s6[0] + s5[2] + s6[1] + t2[2] + s6[2]


def step_of(n):
    g = n // (NB // 2)
    return n % (NB // 2), sum(M_SIZES[:g]), M_SIZES[g]


def s2_units(n):
    return -(-step_of(n)[2] // T_GROUP)


def s2_group(n, u):
    return group(u, -(-step_of(n)[2] // s2_units(n)), step_of(n)[2])


def conv_order():
    mid = []
    for n in range(STEPS + 2):
        if n < STEPS:
            mid += [("S2", n, u) for u in range(s2_units(n))]
        for lag, s in ((1, "S3"), (2, "S4")):
            if 0 <= n - lag < STEPS:
                mid += [(s, n - lag, 0), (s, n - lag, 1)]
    return forward_order() + mid + inverse_order()


def hartley_order():
    def cols(m):
        return range(group(m, 2, KW)[1])
    mid = [("F2", 0, k) for k in cols(0)] + [("CF", 0)]
    for m in range(PAIRS):
        mid += [("TJ", m, 0), ("TJ", m, 1)]
        if m + 1 < PAIRS:
            mid += [("F2", m + 1, k) for k in cols(m + 1)]
        mid += [("H1", m, 0), ("H1", m, 1)]
        if m + 1 < PAIRS:
            mid += [("CF", m + 1)]
        mid += [("H2", m)]
        if m > 0:
            mid += [("CI", m - 1)]
    mid += [("CI", PAIRS - 1)]
    return forward_order() + mid + inverse_order()


class Counts:

    VECTOR = {"S4", "T2", "S6", "CF", "H2"}
    SCALAR = {"S1", "S2", "S3", "F2", "TJ", "H1", "S5 of tile 2"}
    BOTH = {"CI"}

    def __init__(self, order):
        self.order = order
        self.unit, self.by, self.emptied = {}, {}, {}
        self.bank, self.before, holds = {}, {}, {}
        skip = -len(order) % BANKS
        jump = order.index(("T1", 0, 0))
        for n, key in enumerate(order):
            b = (n if n < jump else n + skip) % BANKS
            self.bank[key], self.before[key] = b, holds.get(b)
            holds[b] = key
        self.vec = self.act = 0
        for n, key in enumerate(order):
            self.unit[key] = n
            kinds = {key[0], f"{key[0]} of tile {key[1]}"}
            self.by[key] = (("vec", "act") if kinds & self.BOTH else ("vec",) if kinds & self.VECTOR
                            else ("act",) if kinds & self.SCALAR else (("vec", "act")[key[2] % 2],))
            if "vec" in self.by[key]:
                self.vec += 1
                self.emptied[key, "vec"] = self.vec
            if "act" in self.by[key]:
                self.act += 1
                self.emptied[key, "act"] = self.act
        self.fills = len(order)


def slots():
    return np.array([NT * m + t for t in range(NT) for m in range(TB)])


def constants():
    def cos(a, n):
        return np.cos(2 * np.pi * (a % n) / n).round(17) + 0.0

    def sin(a, n):
        a = a % n
        s = np.sin(2 * np.pi * a / n)
        return np.where((2 * a) % n == 0, 0.0, s)

    k64, h64 = np.arange(64), np.arange(64)
    kw = np.arange(KW)
    cw, sw = cos(np.outer(h64, kw), 64), sin(np.outer(h64, kw), 64)
    dft_w = np.zeros((2, W, 2, 2, KW))
    for j in range(2):
        dft_w[j, :, 0, j] = cw
        dft_w[j, :, 1, j] = -sw
    rows = np.array([2 * hp + j for j in range(2) for hp in range(HP)])
    ch, sh = cos(np.outer(rows, k64), 64), sin(np.outer(rows, k64), 64)
    re, im = np.concatenate([ch, sh]), np.concatenate([-sh, ch])
    dft_h = np.concatenate([re, im], 1)
    flip = -k64 % 64
    dft_h_uv = np.concatenate([(re + im)[:, flip], (im - re)[:, flip]], 1)
    ch, sh = ch.T, sh.T
    zr, zi = np.concatenate([ch, -sh]), np.concatenate([sh, ch])
    inv_h = np.concatenate([zr, zi, zr], 1)
    ch, sh = ch[flip], sh[flip]
    zr, zi = np.concatenate([ch, sh]), np.concatenate([-sh, ch])
    inv_h_dht = np.concatenate([zr, zi, zr + zi], 1)
    inv_w, inv_w_dht = np.zeros((2, 2, Q, 2, W))
    cw, sw = cw.T, sw.T
    for j in range(2):
        for q, k in ((0, 0), (1, 32)):
            inv_w[j, q, j] = cw[k]
            inv_w_dht[j, q, j] = cw[k]
        for k in range(1, 32):
            inv_w[j, 2 * k, j] = 2 * cw[k]
            inv_w[j, 2 * k + 1, j] = -2 * sw[k]
            inv_w_dht[j, 2 * k, j] = cw[k] - sw[k]
            inv_w_dht[j, 2 * k + 1, j] = cw[k] + sw[k]
    tile_c = (NT * np.arange(P)[None, :] + np.arange(NT)[:, None]).ravel()
    block_c = (BS * np.arange(NB)[:, None] + slots()[None, :]).ravel()
    odd = np.zeros(C, bool)
    odd[P // 2 + 1:P], odd[2 * P:] = True, True
    cc = np.outer(tile_c, block_c)
    fwd_c = np.where(odd[:, None], sin(-cc, C), cos(cc, C)).reshape(NT, P, C).transpose(1, 0, 2)
    inv = np.where(odd[:, None], -sin(cc, C), cos(cc, C)).T
    inv = np.concatenate([inv[:, ~odd], inv[:, odd]], 1)
    inv_c = np.zeros((2, HALF, NB // 2, C))
    for b in range(NB):
        inv_c[b % 2, :BS, b // 2] = inv[b * BS:(b + 1) * BS]
    parts = {"identity": np.eye(P), "dft_w": dft_w, "dft_h": dft_h, "dft_h_uv": dft_h_uv, "inv_h": inv_h,
             "inv_h_dht": inv_h_dht, "inv_w": inv_w, "inv_w_dht": inv_w_dht}
    parts = {n: a.reshape(P, -1).astype(np.float32) for n, a in parts.items()}
    return parts, fwd_c.reshape(P, -1).astype(np.float32), inv_c.reshape(P, -1).astype(np.float32)


def build(nc, x, consts, fwd_c_dram, inv_c_dram, conv_w3, conv_w4, conv_bias, l1_w3, l1_w3_bias, l1_q, l1_e, l1_t,
          out, const_at):
    import concourse.bass as bass
    from concourse import mybir
    from contextlib import ExitStack

    F32 = mybir.dt.float32
    F32R = mybir.dt.float32r
    ALU = mybir.AluOpType
    ACT = mybir.ActivationFunctionType
    conv, dht = Counts(conv_order()), Counts(hartley_order())

    ctx = ExitStack()
    with ctx:
        def sb(name, shape):
            return ctx.enter_context(nc.sbuf_tensor(name, shape, F32))

        def sem(name):
            return ctx.enter_context(nc.semaphore(name))

        def dram(name, shape):
            return nc.dram_tensor(name, shape, F32, kind="Internal").ap()

        after_l0 = dram("after_l0", (B, TOK, C))
        l1_sum = dram("l1_sum", (TOK, C))
        second_in = dram("second_in", (TOK, C))
        l1_first = dram("l1_first", (MROWS, NB * MROWS))
        l1_second = dram("l1_second", (MROWS, NB * HALF))

        X = sb("X", [P, NT, HP, P])
        mid_at = nc.sbuf_base
        mid = sb("mid", [P, NB * HALF * KW])
        D = sb("D", [P, KW, C])
        ring_at = nc.sbuf_base
        ring = sb("ring", [P, 2 * P * KW])
        const = sb("const", [P, consts.shape[1]])

        Bpad = mid[:, 0:NB * HALF * KW].rearrange("p (k b s) -> p k b s", b=NB, s=HALF)
        Bpair = mid[:, 0:NB * HALF * KW].rearrange("p (k a n) -> p k a n", a=NB // 2, n=P)
        Bm = mid[:, 0:KW * C].rearrange("p (k c) -> p k c", c=C)
        tables = mid[:, KW * C:KW * C + (NT + NB) * C]

        warm = sb("warm", [P, 2 + NT])

        def cst(name):
            at, n = const_at[name]
            return const[:, at:at + n]

        identity, dft_w, dft_h, dft_h_uv = (cst(n) for n in ("identity", "dft_w", "dft_h", "dft_h_uv"))

        def A(t):
            return ring[:, (t % 2) * P * KW:(t % 2 + 1) * P * KW].rearrange("p (r k) -> p r k", k=KW)

        def E(t):
            at = (t % 2) * P * HP
            return ring[:, at:at + P * HP].rearrange("p (r h) -> p r h", h=HP)

        g_parts = [nc.alloc_sbuf_tensor_at(f"G_{name}", [P, 2 * HP * P], F32R, offset=mid_at + n * 2 * HP * P * 4)
                   for n, name in enumerate(("high", "low"))]
        assert 2 * 2 * HP * P <= NB * HALF * KW
        inv_w_parts = ctx.enter_context(nc.sbuf_tensor("inv_w_parts", [P, 2, 2, P], F32R))

        def G(t, part):
            return g_parts[part][:, (t % 2) * HP * P:(t % 2 + 1) * HP * P]

        def in_ring(sizes):
            at, views = 0, []
            for n in sizes:
                views.append(ring[:, at:at + n])
                at += n
            assert at <= 2 * P * KW
            return views

        W3, W4 = NB * MROWS, NB * 2 * BS
        modes0, modes1, hidden0, hidden1, clip0, clip1, w3, w4, bias = in_ring([2 * BANK] * 4 + [M_GROUP * BS] * 2 + [W3, W4, NB])
        modes, hidden, clip = (modes0, modes1), (hidden0, hidden1), (clip0, clip1)
        assert 4 * 2 * BANK + 2 * M_GROUP * BS >= P * KW
        w3 = w3.rearrange("p (b r) -> p b r", r=MROWS)
        w4 = w4.rearrange("p (b r) -> p b r", r=2 * BS)
        UV, J0, J1, pair0, pair1, hid0, hid1, _, _, _, clip_l1, w3_l1, w4_l1, flipped0, flipped1 = in_ring(
            [NT * P, NB * MROWS, NB * MROWS] + [BANK] * 8 + [NB * MROWS, NB * HALF, C, C])
        assert NT * P + 2 * NB * MROWS + 7 * BANK >= P * KW
        UV = UV.rearrange("p (t n) -> p t n", n=P)
        J = [v.rearrange("p (b r) -> p b r", r=MROWS) for v in (J0, J1)]
        pair, hid, flipped = (pair0, pair1), (hid0, hid1), (flipped0, flipped1)
        shrunk_at = ring_at + (NT * P + 2 * NB * MROWS + 4 * BANK) * 4
        in_turns = [nc.alloc_sbuf_tensor_at(f"shrunk_{n}", [P, BANK], F32R, offset=shrunk_at + n * BANK * 4)
                    for n in range(3)]
        in_turns.append(ctx.enter_context(nc.sbuf_tensor("shrunk_3", [P, BANK], F32R)))
        shrunk = (in_turns[0:2], in_turns[2:4])
        w3_l1 = w3_l1.rearrange("p (b r) -> p b r", r=MROWS)
        w4_l1 = w4_l1.rearrange("p (b r) -> p b r", r=HALF)
        fwd_c = tables[:, 0:NT * C].rearrange("p (t c) -> p t c", c=C)
        inv_c_at = mid_at + (KW + NT) * C * 4
        inv_c_whole = tables[:, (NT + NB // 2) * C:]
        inv_c_parts = [nc.alloc_sbuf_tensor_at(f"inv_c_{name}", [P, NB // 2 * C], F32R,
                                               offset=inv_c_at + n * NB // 2 * C * 4)
                       for n, name in enumerate(("high", "low"))]
        inv_c = [v[:, :].rearrange("p (g c) -> p g c", c=C) for v in inv_c_parts]

        def tile_in_D(t):
            return Dflat[:, t * HP * P:(t + 1) * HP * P]

        def tile_in_X(t):
            return X[:, t].rearrange("p h c -> p (h c)")

        Dflat = D[:, :, :].rearrange("p k c -> p (k c)")
        Xflat = X[:, :, :, :].rearrange("p t h c -> p (t h c)")
        prep, prep_at, at = {}, {}, 0
        for name, n in (("v0", NB * MROWS), ("v1", NB * MROWS), ("v", NB * MROWS), ("q0", NB * MROWS), ("q1", NB * MROWS),
                        ("q", NB * MROWS), ("e0", NB * BS), ("e1", NB * BS), ("d", NB * BS), ("e", NB * BS),
                        ("t0", NB * BS), ("t1", NB * BS), ("w4", NB * HALF)):
            prep[name] = Xflat[:, at:at + n]
            prep_at[name] = at
            at += n

        def load_prep(eng, first, src, loaded):
            parts, n_rows, n = src.shape
            dst = Xflat[0:n_rows, prep_at[first]:prep_at[first] + parts * n]
            eng.dma_start(dst.rearrange("p (a c) -> p a c", c=n), src.rearrange("a p c -> p a c")).then_inc(loaded, 16)

        bank = [ctx.enter_context(nc.psum_tensor(f"bank{i}", [P, BANK], F32)) for i in range(BANKS)]

        filled = sem("filled")
        vec_emptied = sem("vec_emptied")
        act_emptied = sem("act_emptied")
        high_written = sem("high_written")
        matrix_high = sem("matrix_high")
        matrix_low = sem("matrix_low")
        whole_written = sem("whole_written")
        shrunk_high = sem("shrunk_high")
        inv_c_high = sem("inv_c_high")
        inv_c_low = sem("inv_c_low")
        clipped = sem("clipped")
        consts_loaded = sem("consts_loaded")
        prep_loaded = sem("prep_loaded")
        prep_t_loaded = sem("prep_t_loaded")
        prep_v_loaded = sem("prep_v_loaded")
        prep_v_step = sem("prep_v_step")
        prep_step = sem("prep_step")
        prep_product = sem("prep_product")
        prep_stored = sem("prep_stored")
        weights_loaded = sem("weights_loaded")
        weights_signed = sem("weights_signed")
        tables_loaded = sem("tables_loaded")
        l1_weights_loaded = sem("l1_weights_loaded")
        x_loaded = [[sem(f"x_loaded{t}_{c}") for c in range(TILE_PARTS if t == 0 else 1)] for t in range(NT)]
        mixed = [sem(f"mixed{t}") for t in range(NT)]
        differed = [sem(f"differed{t}") for t in range(NT)]
        doubled = sem("doubled")
        stored = [sem(f"stored{t}") for t in range(NT)]
        difference_stored = [sem(f"difference_stored{t}") for t in range(NT)]
        x_free = [sem(f"x_free{t}") for t in range(NT)]
        residual = sem("residual")
        residual_halved = sem("residual_halved")
        pads_zeroed = sem("pads_zeroed")
        pads_written = sem("pads_written")
        flipped_loaded = [sem(f"flipped_loaded{n}") for n in range(2)]
        flipped_placed = sem("flipped_placed")
        subtracted = sem("subtracted")
        folded = sem("folded")
        v_placed = sem("v_placed")

        def wait_stored(eng, t, results, differences):
            if results > 0:
                eng.wait_ge(stored[t], 16 * TILE_PARTS * results)
            if differences > 0:
                eng.wait_ge(difference_stored[t], 16 * differences)

        def part_rows(c):
            return slice(c * HP // TILE_PARTS, (c + 1) * HP // TILE_PARTS)

        def rows(a):
            return a.rearrange("(h p) c -> p h c", p=P)

        class Pass:

            def __init__(self, layer, plan, number, fills, vec, act, copies=None):
                self.t2_units = number * (NT * INV_UNITS)
                self.copies = copies
                self.layer, self.plan = layer, plan
                self.fills, self.vec, self.act = fills, vec + BANKS, act + 1
                self.scale_in = 1.0 if layer in (0, 1) else 0.5 / H
                self.scale_out = [1.0 / TOK, 2.0 / (B * TOK * C), 2.0 / H, 1.0 / H][layer]
                self.inv_h = cst("inv_h_dht" if layer == 1 else "inv_h")
                self.inv_w = inv_w_parts[:, 1 if layer == 1 else 0]

            def bank(self, key):
                return bank[self.plan.bank[key]]

            def fill_of(self, key):
                return self.fills + self.plan.unit[key] + 1

            def wait_filled(self, eng, key):
                eng.wait_ge(filled, self.fill_of(key))

            def wait_emptied(self, eng, *keys):
                for engine, emptied, before in (("vec", vec_emptied, self.vec), ("act", act_emptied, self.act)):
                    counts = [self.plan.emptied[key, engine] for key in keys if engine in self.plan.by[key]]
                    if counts:
                        eng.wait_ge(emptied, before + max(counts))

            def wait_bank(self, pe, key, *others):
                before = self.plan.before[key]
                if before is None:
                    pe.wait_ge(vec_emptied, self.vec - BANKS + self.plan.bank[key] + 1)
                    self.wait_emptied(pe, *others)
                else:
                    self.wait_emptied(pe, *others, before)

            def wait_all(self, eng, stage, t):
                self.wait_emptied(eng, *[key for key in self.plan.order if key[:2] == (stage, t)])

        def pass_l0(i):
            return Pass(0, conv, i, i * conv.fills, i * conv.vec, i * conv.act, i * NT + NT)

        def pass_l1(i):
            return Pass(1, dht, i + 2, i * dht.fills + 2 * conv.fills, i * dht.vec + 2 * conv.vec,
                        i * dht.act + 2 * conv.act, i * NT + (B + 1) * NT)

        def pass_l23(i, layer):
            n = layer - 2
            return Pass(layer, conv, i * 2 + (4 + n), i * (2 * conv.fills) + (2 * conv.fills + 2 * dht.fills + n * conv.fills),
                        i * (2 * conv.vec) + (2 * conv.vec + 2 * dht.vec + n * conv.vec),
                        i * (2 * conv.act) + (2 * conv.act + 2 * dht.act + n * conv.act), i * NT + (2 * B + 1) * NT)

        def mlp_passes_before(i, layer):
            return i if layer == 0 else i * 2 + layer

        CLIPS = 2 * STEPS

        def clips_before(i, layer):
            if layer == 0:
                return i * CLIPS
            if layer == 1:
                return i * PAIRS + 2 * CLIPS
            return i * (2 * CLIPS) + (2 * PAIRS + layer * CLIPS)

        block = ctx.enter_context(nc.Block())

        @block.sync
        def _(sp):
            sp.dma_start(const[:, :], consts).then_inc(consts_loaded, 16)

            def load(src, t):
                dst = tile_in_D(t).rearrange("p (h c) -> p h c", c=P)
                for c, loaded in enumerate(x_loaded[t]):
                    h = part_rows(c) if t == 0 else slice(0, HP)
                    sp.dma_start(dst[:, h], rows(src)[:, h, t * P:(t + 1) * P]).then_inc(loaded, 16)

            def store_difference(n, t):
                sp.wait_ge(differed[t], TILE_PARTS * n)
                sp.dma_start(rows(second_in)[:, :, t * P:(t + 1) * P], X[:, t]).then_inc(difference_stored[t], 16)

            for i in range(B):
                if i > 0:
                    sp.wait_ge(filled, pass_l0(i).fills - TAIL)
                for t in range(NT):
                    load(x[i], t)

            sp.wait_ge(filled, pass_l1(0).fills - TAIL)
            for t in range(NT):
                wait_stored(sp, t, 1, 0)
                load(after_l0[0], t)
            def load_tables(p):
                sp.wait_ge(filled, p.fills)
                sp.dma_start(tables[:, 0:NT * C], fwd_c_dram).then_inc(tables_loaded, 16)
                sp.dma_start(inv_c_whole, inv_c_dram).then_inc(tables_loaded, 16)

            load_tables(pass_l1(0))
            for t in range(NT - 1):
                store_difference(1, t)
            for t in range(NT):
                wait_stored(sp, t, B, 0)
            for i in range(B):
                p = pass_l1(i)
                if i > 0:
                    sp.wait_ge(filled, p.fills - TAIL)
                    for t in range(NT):
                        wait_stored(sp, t, B, 1)
                        load(second_in, t)
                    load_tables(p)
                p.wait_filled(sp, ("T1", 1, T1_UNITS - 1))
                image = after_l0[i].rearrange("(h w) c -> h w c", w=W)
                for m in range(PAIRS):
                    if m >= 2:
                        sp.wait_ge(flipped_placed, i * PAIRS + m - 1)
                    k0, nk = group(m, 2, KW)
                    for k in range(nk):
                        sp.dma_start(flipped[m % 2][k * H:(k + 1) * H], image[:, (W - k0 - k) % W]
                                     ).then_inc(flipped_loaded[m % 2], 16)
                    if i == 0 and m == 1:
                        store_difference(1, NT - 1)

            sp.wait_ge(filled, pass_l23(0, 2).fills - TAIL)
            for t in range(NT):
                wait_stored(sp, t, B + 1, 0)
                load(l1_sum, t)
            for t in range(NT):
                store_difference(2, t)
            for i in range(B):
                p = pass_l23(i, 2)
                if i > 0:
                    sp.wait_ge(filled, p.fills - TAIL)
                    for t in range(NT):
                        wait_stored(sp, t, B + 1, 2)
                        load(second_in, t)

        @block.gpsimd
        def _(pool):
            pool.wait_ge(prep_v_loaded, 16)
            v0, v1, v = (prep[n].rearrange("p (b r) -> p b r", r=MROWS) for n in ("v0", "v1", "v"))
            for part, signs in ((slice(0, HALF), (ALU.add, ALU.subtract)),
                                (slice(HALF, MROWS), (ALU.subtract, ALU.add))):
                for cols, op in zip((slice(0, HALF), slice(HALF, MROWS)), signs):
                    nc.gpsimd.tensor_tensor(v[part, :, cols], v0[part, :, cols], v1[part, :, cols],
                                            op).then_inc(prep_v_step, 1)
            pool.wait_ge(prep_v_step, 4)
            nc.gpsimd.tensor_scalar(prep["v"][0:MROWS], prep["v"][0:MROWS], 0.5, None,
                                    ALU.mult).then_inc(prep_v_step, 1)
            pool.wait_ge(prep_v_step, 5)
            pool.wait_ge(prep_step, PREP_STEPS)
            pool.dma_start(l1_first, prep["v"][0:MROWS]).then_inc(prep_stored, 16)
            pool.dma_start(l1_second, prep["w4"][0:MROWS]).then_inc(prep_stored, 16)
            pool.wait_ge(prep_stored, 32)
            pool.dma_start(l1_first[ONE:ONE + 1], l1_w3_bias).then_inc(prep_stored, 16)

            def free_tiles(results, differences, tiles=range(NT)):
                for t in tiles:
                    wait_stored(pool, t, results, differences)
                    nc.gpsimd.memset(warm[:, 2 + t:3 + t], 0.0).then_inc(x_free[t], 1)

            def store_part(dst, t, c):
                h = part_rows(c)
                pool.dma_start(rows(dst)[:, h, t * P:(t + 1) * P], X[:, t, h]).then_inc(stored[t], 16)

            def mix_first_tile(n):
                for c, loaded in enumerate(x_loaded[0]):
                    pool.wait_ge(loaded, 16 * (B * n + 1))
                    h = part_rows(c)
                    d = tile_in_D(0)[:, h.start * P:h.stop * P]
                    nc.gpsimd.tensor_tensor(d, d, tile_in_X(0)[:, h.start * P:h.stop * P],
                                            ALU.add).then_inc(mixed[0], 1)

            def store(p, dst, results, differences, mix=None):
                for t in range(NT):
                    for c in range(TILE_PARTS):
                        p.wait_emptied(pool, ("S6", t, (c + 1) * INV_UNITS // TILE_PARTS - 1))
                        store_part(dst, t, c)
                    if mix is not None and t == 0:
                        mix_first_tile(mix)
                free_tiles(results, differences)

            def make_difference(n):
                for t in range(VECTOR_DIFFS, NT):
                    pool.wait_ge(mixed[t], n)
                    if n == 1:
                        pool.wait_ge(x_free[t], B + 1)
                    for c in range(TILE_PARTS):
                        h = part_rows(c)
                        cols = slice(h.start * P, h.stop * P)
                        part = tile_in_X(t)[:, cols]
                        nc.gpsimd.tensor_scalar(part, part, -2.0, None, ALU.mult).then_inc(doubled, 1)
                        parts = (NT - VECTOR_DIFFS) * TILE_PARTS * (n - 1) + (t - VECTOR_DIFFS) * TILE_PARTS + c + 1
                        pool.wait_ge(doubled, parts)
                        nc.gpsimd.tensor_tensor(part, part, tile_in_D(t)[:, cols], ALU.add).then_inc(differed[t], 1)

            def zero_pads(p):
                if p.fills > 0:
                    pool.wait_ge(filled, p.fills)
                nc.gpsimd.memset(Bpad[:, :, :, BS:], 0.0).then_inc(pads_zeroed, 1)

            pool.wait_ge(prep_stored, 48)
            free_tiles(0, 0)
            for i in range(B):
                zero_pads(pass_l0(i))
                store(pass_l0(i), after_l0[i], i + 1, 0, 1 if i == B - 1 else None)
            make_difference(1)
            for i in range(B):
                p = pass_l1(i)
                p.wait_filled(pool, ("T1", NT - 1, T1_UNITS - 1))
                for m in range(PAIRS):
                    k0, nk = group(m, 2, KW)
                    columns = [sum(group(n, 2, KW)[1] for n in range(m % 2, end, 2)) for end in (m + 1, PAIRS)]
                    pool.wait_ge(flipped_loaded[m % 2], 16 * (i * columns[1] + columns[0]))
                    if m >= 2:
                        p.wait_filled(pool, ("TJ", m - 2, 1))
                    n = nk * H
                    nc.gpsimd.tensor_copy(
                        J[m % 2][0:n, :, HALF:MROWS].rearrange("p b (t c) -> p b t c", t=NT),
                        flipped[m % 2][0:n].rearrange("p (t b c) -> p b t c", t=NT, b=NB)).then_inc(flipped_placed, 1)
                    if i == 0 and m < 2:
                        free_tiles(B, 1, range(NT - 1) if m == 0 else [NT - 1])
                if i == 0:
                    store(p, l1_sum, B + 1, 1)
                else:
                    p.wait_emptied(pool, ("S6", 0, INV_UNITS - 1))
                    mix_first_tile(2)
            for i in range(B):
                zero_pads(pass_l23(i, 2))
                if i == 0:
                    make_difference(2)
                    free_tiles(B + 1, 2)
                zero_pads(pass_l23(i, 3))
                p = pass_l23(i, 3)
                p.wait_filled(pool, ("S1", NT - 1, S1_UNITS - 1))
                nc.gpsimd.tensor_scalar(X[:, :, :, :].rearrange("p t h c -> p (t h c)"),
                                        X[:, :, :, :].rearrange("p t h c -> p (t h c)"), 0.5, None,
                                        ALU.mult).then_inc(residual_halved, 1)
                store(pass_l23(i, 3), out[i], B + 2 + i, 2)

        @block.tensor
        def _(pe):
            def forward(p, x_ready):
                def s1(t):
                    parts = 0
                    for g in range(S1_UNITS):
                        key = ("S1", t, g)
                        h0, nh = group(g, S1_GROUP, HP)
                        while parts < len(x_loaded[t]) and (t > 0 or part_rows(parts).start < h0 + nh):
                            x_ready(t, parts)
                            parts += 1
                        p.wait_bank(pe, key)
                        for k in range(nh):
                            n = 4 * KW
                            lhsT = X[:, t, h0 + k] if p.layer == 3 else tile_in_D(t)[:, (h0 + k) * P:(h0 + k + 1) * P]
                            mm = nc.tensor.matmul(p.bank(key)[:, k * n:(k + 1) * n], lhsT, dft_w,
                                                  start=True, stop=True)
                        mm.then_inc(filled, 1)

                def t1(t):
                    p.wait_all(pe, "S1", t)
                    for g in range(T1_UNITS):
                        key = ("T1", t, g)
                        p.wait_bank(pe, key)
                        k0, nk = group(g, T_GROUP, KW)
                        for k in range(nk):
                            mm = nc.tensor.transpose(p.bank(key)[:, k * P:(k + 1) * P], A(t)[:, :, k0 + k], identity)
                        mm.then_inc(filled, 1)

                s1(0)
                s1(1)
                t1(0)
                s1(2)
                t1(1)
                t1(2)

            def inverse(p):
                def s5(t):
                    for u in S5_ORDER:
                        key = ("S5", t, u)
                        kws = [0, KW - 1, 1, 2, 3] if u == 0 else range(4 * u, 4 * u + 4)
                        steps = [n for n in range(STEPS) if n % (NB // 2) == NB // 2 - 1
                                 and step_of(n)[1] <= max(kws)]
                        result = ("CI", max(kws) // 2) if p.layer == 1 else ("S4", steps[-1], 1)
                        p.wait_bank(pe, key, *([result] if t == 0 else []))
                        at = 0
                        for k in kws:
                            rhs = p.inv_h[:, 2 * H:3 * H] if k in (0, KW - 1) else p.inv_h[:, 0:2 * H]
                            n = rhs.shape[1]
                            mm = nc.tensor.matmul(p.bank(key)[:, at:at + n], D[:, k, t * P:(t + 1) * P], rhs,
                                                  start=True, stop=True)
                            at += n
                        mm.then_inc(filled, 1)

                def t2(t):
                    p.wait_all(pe, "S5", t)
                    for u in range(INV_UNITS):
                        key = ("T2", t, u)
                        p.wait_bank(pe, key)
                        for k in range(T_GROUP):
                            mm = nc.tensor.transpose(p.bank(key)[:, k * P:(k + 1) * P], E(t)[:, :, u * T_GROUP + k],
                                                     identity)
                        mm.then_inc(filled, 1)

                def s6(t):
                    if t == 0:
                        pe.wait_ge(matrix_low, 2)
                    for u in range(INV_UNITS):
                        key = ("S6", t, u)
                        p.wait_bank(pe, key, ("T2", t, u))
                        products = ((0, 0), (1, 0), (0, 1))
                        for n, (matrix, g) in enumerate(products):
                            mm = nc.tensor.matmul(p.bank(key)[:, :], p.inv_w[:, matrix],
                                                  G(t, g)[:, u * BANK:(u + 1) * BANK],
                                                  start=n == 0, stop=n == len(products) - 1)
                        mm.then_inc(filled, 1)

                s5(0)
                s5(1)
                t2(0)
                t2(1)
                s6(0)
                s5(2)
                s6(1)
                t2(2)
                s6(2)

            def mlp(p, i):
                def s2(n):
                    a, k0, nk = step_of(n)
                    for u in range(s2_units(n)):
                        key = ("S2", n, u)
                        at, cols = s2_group(n, u)
                        units = sorted({(k0 + at) // T_GROUP, (k0 + at + cols - 1) // T_GROUP})
                        p.wait_bank(pe, key, *([("T1", NT - 1, g) for g in units] if a == 0 else []))
                        for k in range(cols):
                            mm = nc.tensor.matmul(p.bank(key)[:, k * P:(k + 1) * P], Bpair[:, k0 + at + k, a], dft_h,
                                                  start=True, stop=True)
                        mm.then_inc(filled, 1)

                def s3(n):
                    a, _, nk = step_of(n)
                    p.wait_emptied(pe, ("S2", n, s2_units(n) - 1))
                    for b in range(2):
                        key = ("S3", n, b)
                        p.wait_bank(pe, key)
                        nc.tensor.matmul(p.bank(key)[0:MROWS, 0:nk * H], w3[:, 2 * a + b],
                                         modes[n % 2][:, b * BANK:b * BANK + nk * H],
                                         start=True, stop=True).then_inc(filled, 1)

                def s4(n):
                    a, _, nk = step_of(n)
                    for b in range(2):
                        key = ("S4", n, b)
                        p.wait_bank(pe, key)
                        p.wait_emptied(pe, ("S3", n, b))
                        for k in range(-(-nk // 2)):
                            mm = nc.tensor.matmul(p.bank(key)[:, k * 2 * BS:(k + 1) * 2 * BS],
                                                  hidden[n % 2][0:MROWS, b * BANK + k * P:b * BANK + (k + 1) * P],
                                                  w4[0:MROWS, 2 * a + b], start=True, stop=True)
                        mm.then_inc(filled, 1)

                passes = mlp_passes_before(i, p.layer)
                pe.wait_ge(pads_zeroed, passes + 1)
                for n in range(STEPS + 2):
                    if n < STEPS:
                        s2(n)
                    if n == 1:
                        pe.wait_ge(weights_signed, passes * 2 + 2)
                    if 0 <= n - 1 < STEPS:
                        s3(n - 1)
                    if 0 <= n - 2 < STEPS:
                        s4(n - 2)

            def hartley(p, i):
                def f2(m):
                    k0, nk = group(m, 2, KW)
                    pe.wait_ge(folded, i * PAIRS + (m + 1))
                    for k in range(nk):
                        key = ("F2", m, k)
                        p.wait_bank(pe, key)
                        for t in range(NT):
                            mm = nc.tensor.matmul(p.bank(key)[:, t * P:(t + 1) * P], Bm[:, k0 + k, t * P:(t + 1) * P],
                                                  dft_h_uv, start=True, stop=True)
                        mm.then_inc(filled, 1)

                def cf(m):
                    key, nk = ("CF", m), group(m, 2, KW)[1]
                    p.wait_bank(pe, key)
                    p.wait_emptied(pe, ("F2", m, nk - 1))
                    for t in range(NT):
                        mm = nc.tensor.matmul(p.bank(key)[0:nk * H, 0:C], UV[:, t, 0:nk * H], fwd_c[:, t],
                                              start=t == 0, stop=t == NT - 1)
                    mm.then_inc(filled, 1)

                def tj(m):
                    p.wait_emptied(pe, ("CF", m))
                    pe.wait_ge(flipped_placed, i * PAIRS + (m + 1))
                    for half in range(2):
                        key = ("TJ", m, half)
                        p.wait_bank(pe, key)
                        for b in range(4):
                            mm = nc.tensor.transpose(p.bank(key)[0:MROWS, b * P:(b + 1) * P], J[m % 2][:, half * 4 + b],
                                                     identity)
                        mm.then_inc(filled, 1)

                def h1(m):
                    nk = group(m, 2, KW)[1]
                    for half in range(2):
                        key = ("H1", m, half)
                        p.wait_bank(pe, key)
                        p.wait_emptied(pe, ("TJ", m, half))
                        for b in range(4):
                            mm = nc.tensor.matmul(p.bank(key)[0:MROWS, b * P:b * P + nk * H],
                                                  w3_l1[0:MROWS, half * 4 + b], pair[half][0:MROWS, b * P:b * P + nk * H],
                                                  start=True, stop=True)
                        mm.then_inc(filled, 1)

                def h2(m):
                    key, nk = ("H2", m), group(m, 2, KW)[1]
                    p.wait_bank(pe, key)
                    p.wait_emptied(pe, ("H1", m, 1))
                    for b in range(NB):
                        row, g = b % 2 * HALF, b // 2
                        mm = nc.tensor.matmul(p.bank(key)[row:row + HALF, g * P:g * P + nk * H], w4_l1[0:MROWS, b],
                                              hid[b // 4][0:MROWS, b % 4 * P:b % 4 * P + nk * H],
                                              start=True, stop=True)
                    mm.then_inc(filled, 1)

                def ci(m):
                    key, n = ("CI", m), group(m, 2, KW)[1] * H
                    p.wait_bank(pe, key)
                    p.wait_emptied(pe, ("H2", m))
                    products = [(g, a, b) for g in range(NB // 2) for a, b in ((0, 0), (1, 0), (0, 1))]
                    for at, (g, a, b) in enumerate(products):
                        mm = nc.tensor.matmul(p.bank(key)[0:n, 0:C], shrunk[m % 2][a][:, g * P:g * P + n],
                                              inv_c[b][:, g], start=at == 0, stop=at == len(products) - 1)
                    mm.then_inc(filled, 1)

                f2(0)
                pe.wait_ge(tables_loaded, i * 32 + 32)
                cf(0)
                pe.wait_ge(pads_written, i * 2 + 2)
                pe.wait_ge(l1_weights_loaded, i * 32 + 32)
                for m in range(PAIRS):
                    tj(m)
                    if m + 1 < PAIRS:
                        f2(m + 1)
                    h1(m)
                    if m + 1 < PAIRS:
                        cf(m + 1)
                    h2(m)
                    if m == 1:
                        pe.wait_ge(inv_c_low, i + 1)
                    if m > 0:
                        ci(m - 1)
                ci(PAIRS - 1)

            pe.wait_ge(prep_step, PREP_OPERANDS)
            for b in range(NB):
                mm = nc.tensor.matmul(bank[BANKS - 1][0:MROWS, b * BS:(b + 1) * BS],
                                      prep["q"][0:BS, b * MROWS:(b + 1) * MROWS], prep["e"][0:BS, b * BS:(b + 1) * BS],
                                      start=True, stop=True)
            mm.then_inc(prep_product, 1)
            pe.wait_ge(consts_loaded, 16)

            with pe.Fori(0, B) as i:
                p = pass_l0(i)
                forward(p, lambda t, c: pe.wait_ge(x_loaded[t][c], i * 16 + 16))
                mlp(p, i)
                inverse(p)

            def joined(t, c, n, loads):
                pe.wait_ge(mixed[t], (n - 1) * len(x_loaded[t]) + c + 1)
                pe.wait_ge(x_loaded[t][c], loads)

            with pe.Fori(0, B) as i:
                p = pass_l1(i)
                forward(p, lambda t, c: joined(t, c, 1, i * 16 + 16 * (B + 1)))
                hartley(p, i)
                inverse(p)
            with pe.Fori(0, B) as i:
                p = pass_l23(i, 2)
                forward(p, lambda t, c: joined(t, c, 2, i * 16 + 16 * (2 * B + 1)))
                mlp(p, i)
                inverse(p)
                p = pass_l23(i, 3)
                forward(p, lambda t, c: None)
                mlp(p, i)
                inverse(p)

        def empty_forward(p, eng, me, copy, emptied, between=None):
            for key in p.plan.order:
                if key[0] not in ("S1", "T1") or me not in p.plan.by[key]:
                    continue
                stage, t, g = key
                p.wait_filled(eng, key)
                if stage == "S1":
                    h0, nh = group(g, S1_GROUP, HP)
                    dst = A(t)[:, :, :].rearrange("p (a h) k -> p h a k", h=HP)[:, h0:h0 + nh]
                    src = p.bank(key)[:, 0:nh * 4 * KW].rearrange("p (h a k) -> p h a k", a=4, k=KW)
                else:
                    k0, nk = group(g, T_GROUP, KW)
                    if p.layer == 1:
                        dst = Bm[:, k0:k0 + nk, t * P:(t + 1) * P]
                        src = p.bank(key)[:, 0:nk * P].rearrange("p (k c) -> p k c", c=P)
                    else:
                        dst = Bpad[:, k0:k0 + nk, :, t * TB:(t + 1) * TB]
                        src = p.bank(key)[:, 0:nk * P].rearrange("p (k b c) -> p k b c", b=NB, c=TB)
                copy(dst, src).then_inc(emptied, 1)
                if between is not None:
                    between(key)

        def empty_inverse(p, eng, me, copy, emptied):
            for key in p.plan.order:
                if key[0] not in ("S5", "T2", "S6") or (me not in p.plan.by[key] and key[0] != "T2"):
                    continue
                stage, t, u = key
                p.wait_filled(eng, key)
                if stage == "S5":
                    dst = E(t).rearrange("p (j q) h -> p q j h", j=2)[:, 8 * u:8 * u + 8]
                    copy(dst, p.bank(key)[:, :].rearrange("p (q j h) -> p q j h", j=2, h=HP)).then_inc(emptied, 1)
                elif stage == "T2":
                    high, low = (G(t, part)[:, u * BANK:(u + 1) * BANK] for part in range(2))
                    if me == "act":
                        copy(high, p.bank(key)[:, :]).then_inc(high_written, 1)
                    else:
                        eng.wait_ge(high_written, p.t2_units + (t * INV_UNITS + u + 1))
                        nc.vector.tensor_tensor(low, p.bank(key)[:, :], high, ALU.subtract).then_inc(emptied, 1)
                else:
                    rows4 = X[:, t, 4 * u:4 * u + 4].rearrange("p h c -> p (h c)")
                    nc.vector.scalar_tensor_tensor(out=rows4, in0=p.bank(key)[:, :], scalar=p.scale_out, in1=rows4,
                                                   op0=ALU.mult, op1=ALU.add).then_inc(emptied, 1)

        @block.scalar
        def _(act):
            def copy(dst, src):
                return nc.scalar.activation(dst, src, ACT.Copy)

            def load_weights(p, key):
                if key != ("T1", NT - 1, 1):
                    return
                p.wait_filled(act, ("T1", 1, T1_UNITS - 1))
                if p.layer == 1:
                    act.wait_ge(prep_stored, 48)
                    for dst, src in ((w3_l1, l1_first), (w4_l1, l1_second)):
                        act.dma_start(dst[0:MROWS].rearrange("p b r -> p (b r)"), src).then_inc(l1_weights_loaded, 16)
                else:
                    n = (0, None, 1, 2)[p.layer]
                    act.dma_start(w3, conv_w3[n]).then_inc(weights_loaded, 16)
                    act.dma_start(w4[0:MROWS], conv_w4[n]).then_inc(weights_loaded, 16)
                    act.dma_start(bias[0:MROWS], conv_bias[n]).then_inc(weights_loaded, 16)

            def mlp(p, i):
                for n in range(STEPS + 1):
                    if n < STEPS:
                        _, _, nk = step_of(n)
                        for u in range(s2_units(n)):
                            key = ("S2", n, u)
                            at, cols = s2_group(n, u)
                            p.wait_filled(act, key)
                            for b in range(2):
                                src = p.bank(key)[b * HALF:(b + 1) * HALF, 0:cols * P].rearrange(
                                    "p (k a h) -> p k a h", a=2, h=H)
                                for ri in range(2):
                                    lo = b * BANK + at * H
                                    dst = modes[n % 2][ri * HALF:(ri + 1) * HALF, lo:lo + cols * H]
                                    moved = nc.scalar.activation(dst.rearrange("p (k h) -> p k h", h=H),
                                                                 src[:, :, ri], ACT.Copy, scale=p.scale_in)
                            moved.then_inc(act_emptied, 1)
                    if n == 0:
                        act.wait_ge(weights_loaded, mlp_passes_before(i, p.layer) * 48 + 48)
                    if n > 0:
                        a, _, nk = step_of(n - 1)
                        for b in range(2):
                            key, lo, blk = ("S3", n - 1, b), b * BANK, 2 * a + b
                            p.wait_filled(act, key)
                            nc.scalar.activation(hidden[(n - 1) % 2][0:MROWS, lo:lo + nk * H],
                                                 p.bank(key)[0:MROWS, 0:nk * H], ACT.Relu,
                                                 bias=bias[0:MROWS, blk:blk + 1]).then_inc(act_emptied, 1)

            def hartley(p, i):
                def f2(m):
                    for k in range(group(m, 2, KW)[1]):
                        key = ("F2", m, k)
                        p.wait_filled(act, key)
                        cols = slice(k * H, (k + 1) * H)
                        src = p.bank(key)[:, 0:NT * P].rearrange("p (t a n) -> p t a n", a=2, n=H)
                        copy(UV[HALF:P, 0, cols], src[HALF:P, 0, 1]).then_inc(v_placed, 1)
                        copy(UV[0:HALF, 0, cols], src[0:HALF, 0, 0])
                        copy(UV[:, 1, cols], src[:, 1, 0])
                        copy(UV[:, 2, cols], src[:, 2, 1])
                        act.wait_ge(v_placed, i * KW + (2 * m + k + 1))
                        copy(UV[HALF:MIDDLE, 0, cols], src[HALF:MIDDLE, 0, 0]).then_inc(act_emptied, 1)

                def ci(m):
                    key = ("CI", m)
                    p.wait_filled(act, key)
                    k0, nk = group(m, 2, KW)
                    for k in range(nk):
                        src, dst = p.bank(key)[k * H:(k + 1) * H, 0:EVEN], D[0:H, k0 + k]
                        copy(dst[:, 0:MIDDLE], src[:, 0:MIDDLE])
                        copy(dst[:, P:2 * P], src[:, MIDDLE:])
                        copy(dst[:, P - 1:P - MIDDLE + 1:-1], src[:, 1:MIDDLE - 1])
                        last = copy(dst[:, C - 1:2 * P - 1:-1], src[:, MIDDLE:])
                    last.then_inc(act_emptied, 1)

                f2(0)
                for m in range(PAIRS):
                    n = group(m, 2, KW)[1] * H
                    for half in range(2):
                        key = ("TJ", m, half)
                        p.wait_filled(act, key)
                        copy(pair[half][0:MROWS].rearrange("p (b n) -> p b n", n=P)[:, :, 0:n],
                             p.bank(key)[0:MROWS].rearrange("p (b n) -> p b n", n=P)[:, :, 0:n]).then_inc(act_emptied, 1)
                    if m + 1 < PAIRS:
                        f2(m + 1)
                    for half in range(2):
                        key = ("H1", m, half)
                        p.wait_filled(act, key)
                        nc.scalar.activation(hid[half][0:MROWS].rearrange("p (b n) -> p b n", n=P)[:, :, 0:n],
                                             p.bank(key)[0:MROWS].rearrange("p (b n) -> p b n", n=P)[:, :, 0:n],
                                             ACT.Relu).then_inc(act_emptied, 1)
                    if m == 1:
                        act.wait_ge(residual, p.copies)
                    if m > 0:
                        ci(m - 1)
                ci(PAIRS - 1)

            load_prep(act, "q0", l1_q, prep_loaded)
            load_prep(act, "e0", l1_e, prep_loaded)
            act.wait_ge(x_loaded[0][0], 16)
            load_prep(act, "t0", l1_t, prep_t_loaded)
            load_prep(act, "v0", l1_w3, prep_v_loaded)
            act.wait_ge(vec_emptied, BANKS - 1)
            nc.scalar.activation(warm[:, 1:2], warm[:, 0:1], ACT.Relu).then_inc(act_emptied, 1)
            with act.Fori(0, B) as i:
                p = pass_l0(i)
                empty_forward(p, act, "act", copy, act_emptied, lambda key: load_weights(p, key))
                mlp(p, i)
                empty_inverse(p, act, "act", copy, act_emptied)
            with act.Fori(0, B) as i:
                p = pass_l1(i)
                empty_forward(p, act, "act", copy, act_emptied, lambda key: load_weights(p, key))
                hartley(p, i)
                empty_inverse(p, act, "act", copy, act_emptied)
            with act.Fori(0, B) as i:
                for layer in (2, 3):
                    p = pass_l23(i, layer)
                    empty_forward(p, act, "act", copy, act_emptied, lambda key: load_weights(p, key))
                    mlp(p, i)
                    empty_inverse(p, act, "act", copy, act_emptied)

        @block.vector
        def _(vec):
            def copy(dst, src):
                return nc.vector.tensor_copy(dst, src)

            def clip_to(p, key, held, src, clips, done):
                p.wait_filled(vec, key)
                if done is not None:
                    vec.wait_ge(vec_emptied, p.vec + done)
                nc.vector.tensor_scalar(held, src, -LAMBDA, LAMBDA, ALU.max, ALU.min).then_inc(clipped, 1)
                vec.wait_ge(clipped, clips)

            def set_signs(p, i):
                vec.wait_ge(weights_loaded, mlp_passes_before(i, p.layer) * 48 + 48)
                for w, end in ((w3, P), (w4, MROWS)):
                    nc.vector.tensor_scalar(w[HALF:end, :, 0:BS], w[HALF:end, :, 0:BS], -1.0, None,
                                            ALU.mult).then_inc(weights_signed, 1)

            def copy_residual(p, t, frees, loads, mixes):
                vec.wait_ge(x_free[t], frees)
                for loaded in x_loaded[t]:
                    vec.wait_ge(loaded, loads)
                if mixes:
                    vec.wait_ge(mixed[t], mixes * len(x_loaded[t]))
                nc.vector.tensor_copy(tile_in_X(t), tile_in_D(t)).then_inc(residual, 1)

            def mlp(p, i, copy_input=None):
                set_signs(p, i)
                if copy_input is not None:
                    for t in range(NT):
                        copy_input(t)
                vec.wait_ge(residual, p.copies)
                clips = clips_before(i, p.layer)
                Dtiles = D[:, :, :].rearrange("p k (t b c) -> p k t b c", t=NT, b=NB)
                for n in range(STEPS):
                    a, k0, nk = step_of(n)
                    pairs = -(-nk // 2)
                    for b in range(2):
                        key = ("S4", n, b)
                        cols = pairs * 2 * BS
                        src, held = p.bank(key)[:, 0:cols], clip[b][:, 0:cols]
                        clip_to(p, key, held, src, clips + (2 * n + b + 1),
                                p.plan.emptied[("S4", n - 1, b), "vec"] if n else None)
                        src, held = (v.rearrange("p (k a t c) -> p k a t c", a=2, t=NT, c=TB) for v in (src, held))
                        for part in range(2):
                            half, n_of_part = slice(part * H, (part + 1) * H), (nk + 1 - part) // 2
                            for ri in range(2):
                                dst = Dtiles[ri * H:(ri + 1) * H, k0 + part:k0 + nk:2, :, 2 * a + b]
                                moved = nc.vector.tensor_tensor(dst, src[half, 0:n_of_part, ri], held[half, 0:n_of_part, ri],
                                                                ALU.subtract)
                        moved.then_inc(vec_emptied, 1)

            def fold(p, i, m):
                k0, nk = group(m, 2, KW)
                p.wait_emptied(vec, ("T1", NT - 1, (k0 + nk - 1) // T_GROUP))
                b = Bm[:, k0:k0 + nk]
                ranges = ((b[:, :, 1:P - MIDDLE + 1], b[:, :, P - 1:MIDDLE - 1:-1]),
                          (b[:, :, P:2 * P], b[:, :, C - 1:2 * P - 1:-1]))
                for low, high in ranges:
                    nc.vector.tensor_tensor(high, low, high, ALU.subtract).then_inc(subtracted, 1)
                vec.wait_ge(subtracted, i * (2 * PAIRS) + (2 * m + 2))
                for low, high in ranges:
                    last = nc.vector.scalar_tensor_tensor(out=low, in0=low, scalar=2.0, in1=high,
                                                          op0=ALU.mult, op1=ALU.subtract)
                last.then_inc(folded, 1)

            def split_inv_c(i):
                vec.wait_ge(tables_loaded, i * 32 + 32)
                copy(inv_c_parts[0][:, :], inv_c_whole).then_inc(inv_c_high, 1)
                vec.wait_ge(inv_c_high, i + 1)
                nc.vector.tensor_tensor(inv_c_parts[1][:, :], inv_c_whole, inv_c_parts[0][:, :],
                                        ALU.subtract).then_inc(inv_c_low, 1)

            def hartley(p, i, copy_input):
                clips = clips_before(i, 1)
                p.wait_filled(vec, ("T1", NT - 1, T1_UNITS - 1))
                both = ring[:, NT * P:NT * P + 2 * NB * MROWS].rearrange("p (b r) -> p b r", r=MROWS)
                nc.vector.memset(both[:, :, ONE:ONE + 1], 1.0).then_inc(pads_written, 1)
                nc.vector.memset(both[:, :, ONE + 1:HALF], 0.0).then_inc(pads_written, 1)

                def cf(m):
                    key, n = ("CF", m), group(m, 2, KW)[1] * H
                    p.wait_filled(vec, key)
                    copy(J[m % 2][0:n, :, 0:BS],
                         p.bank(key)[0:n, 0:C].rearrange("p (b c) -> p b c", c=BS)).then_inc(vec_emptied, 1)

                def ci(m):
                    key = ("CI", m)
                    p.wait_filled(vec, key)
                    vec.wait_ge(act_emptied, p.act + p.plan.emptied[key, "act"])
                    k0, nk = group(m, 2, KW)
                    for k in range(nk):
                        src, dst = p.bank(key)[k * H:(k + 1) * H, EVEN:C], D[H:P, k0 + k]
                        copy(dst[:, MIDDLE:P], src[:, 0:P - MIDDLE])
                        copy(dst[:, 2 * P:], src[:, P - MIDDLE:])
                        nc.vector.tensor_scalar(dst[:, P - MIDDLE:0:-1], src[:, 0:P - MIDDLE], -1.0, None, ALU.mult)
                        last = nc.vector.tensor_scalar(dst[:, 2 * P - 1:P - 1:-1], src[:, P - MIDDLE:], -1.0, None,
                                                       ALU.mult)
                    last.then_inc(vec_emptied, 1)

                cf(0)
                for t in range(NT - 1):
                    copy_input(t)
                for m in range(PAIRS):
                    if m + 1 < PAIRS:
                        cf(m + 1)
                    if m + 2 < PAIRS:
                        fold(p, i, m + 2)
                    key, n = ("H2", m), group(m, 2, KW)[1] * H
                    src, held, high, low = (v.rearrange("p (g n) -> p g n", n=P)[:, :, 0:n] for v in
                                            (p.bank(key)[:, :], clip_l1, *(v[:, :] for v in shrunk[m % 2])))
                    clip_to(p, key, held, src, clips + (m + 1), p.plan.emptied[("H2", m - 1), "vec"] if m else None)
                    nc.vector.tensor_tensor(held, src, held, ALU.subtract).then_inc(whole_written, 1)
                    vec.wait_ge(whole_written, i * PAIRS + (m + 1))
                    copy(high, held).then_inc(shrunk_high, 1)
                    vec.wait_ge(shrunk_high, i * PAIRS + (m + 1))
                    nc.vector.tensor_tensor(low, held, high, ALU.subtract).then_inc(vec_emptied, 1)
                    if m == 0:
                        copy_input(NT - 1)
                        vec.wait_ge(residual, p.copies)
                        for c in (0, MIDDLE - 1):
                            nc.vector.memset(D[H:P, :, c:c + 1], 0.0)
                    if m > 0:
                        ci(m - 1)
                ci(PAIRS - 1)

            def mix(n, last):
                for t in range(1, NT):
                    last.wait_emptied(vec, ("S6", t, INV_UNITS - 1))
                    vec.wait_ge(x_loaded[t][0], 16 * (B * n + 1))
                    nc.vector.tensor_tensor(tile_in_D(t), tile_in_D(t), tile_in_X(t), ALU.add).then_inc(mixed[t], 1)
                for t in range(VECTOR_DIFFS):
                    vec.wait_ge(mixed[t], n * len(x_loaded[t]))
                    if n == 1:
                        vec.wait_ge(x_free[t], B + 1)
                    nc.vector.scalar_tensor_tensor(out=tile_in_X(t), in0=tile_in_X(t), scalar=-2.0, in1=tile_in_D(t),
                                                   op0=ALU.mult, op1=ALU.add).then_inc(differed[t], TILE_PARTS)

            nc.vector.memset(warm[:, 0:1], 0.0).then_inc(vec_emptied, BANKS - 1)

            steps = 0

            def step(ins):
                nonlocal steps
                steps += 1
                ins.then_inc(prep_step, 1)

            def after_steps():
                vec.wait_ge(prep_step, steps)

            def blocks(name, r):
                return prep[name].rearrange("p (b r) -> p b r", r=r)

            vec.wait_ge(prep_loaded, 2 * 16)
            q0, q1, q = (blocks(n, MROWS) for n in ("q0", "q1", "q"))
            step(nc.vector.tensor_tensor(q[0:BS, :, 0:HALF], q0[0:BS, :, 0:HALF], q1[0:BS, :, 0:HALF], ALU.add))
            step(nc.vector.tensor_tensor(q[0:BS, :, HALF:], q0[0:BS, :, HALF:], q1[0:BS, :, HALF:], ALU.subtract))
            step(nc.vector.tensor_tensor(prep["e"][0:BS], prep["e0"][0:BS], prep["e1"][0:BS], ALU.subtract))
            after_steps()
            step(nc.vector.tensor_scalar(q[0:BS, :, 0:BS], q[0:BS, :, 0:BS], 0.5, None, ALU.mult))
            step(nc.vector.tensor_scalar(q[0:BS, :, HALF:], q[0:BS, :, HALF:], 0.5, None, ALU.mult))
            step(nc.vector.scalar_tensor_tensor(out=prep["e"][0:BS], in0=prep["e"][0:BS], scalar=0.5,
                                                in1=prep["d"][0:BS], op0=ALU.mult, op1=ALU.add))
            assert steps == PREP_OPERANDS
            step(nc.vector.memset(prep["w4"][0:MROWS], 0.0))
            after_steps()
            vec.wait_ge(prep_product, 1)
            w4_new = blocks("w4", HALF)[0:MROWS, :, 0:BS]
            nc.vector.tensor_copy(w4_new, bank[BANKS - 1][0:MROWS, 0:NB * BS].rearrange("p (b c) -> p b c", c=BS)
                                  ).then_inc(vec_emptied, 1)
            vec.wait_ge(vec_emptied, BANKS)
            t0, t1 = prep["t0"], prep["t1"]
            vec.wait_ge(prep_t_loaded, 16)
            step(nc.vector.tensor_tensor(t0[0:MROWS], t0[0:MROWS], t1[0:MROWS], ALU.add))
            after_steps()
            step(nc.vector.tensor_scalar(t0[HALF:MROWS], t0[HALF:MROWS], 0.5, None, ALU.mult))
            after_steps()
            step(nc.vector.tensor_tensor(w4_new, w4_new, blocks("t0", BS)[0:MROWS], ALU.add))
            assert steps == PREP_STEPS

            vec.wait_ge(consts_loaded, 16)
            for n, name in enumerate(("inv_w", "inv_w_dht")):
                nc.vector.tensor_copy(inv_w_parts[:, n, 0], cst(name)).then_inc(matrix_high, 1)
            vec.wait_ge(matrix_high, 2)
            for n, name in enumerate(("inv_w", "inv_w_dht")):
                nc.vector.tensor_tensor(inv_w_parts[:, n, 1], cst(name), inv_w_parts[:, n, 0],
                                        ALU.subtract).then_inc(matrix_low, 1)

            with vec.Fori(0, B) as i:
                p = pass_l0(i)
                empty_forward(p, vec, "vec", copy, vec_emptied)
                mlp(p, i, lambda t: copy_residual(p, t, i + 1, i * 16 + 16, 0))
                empty_inverse(p, vec, "vec", copy, vec_emptied)
            mix(1, pass_l0(1))
            with vec.Fori(0, B) as i:
                p = pass_l1(i)
                def between(key):
                    if key == ("T1", 0, T1_UNITS - 1):
                        split_inv_c(i)
                    if key in (("T1", NT - 1, 2), ("T1", NT - 1, 4)):
                        fold(p, i, key[2] // 2 - 1)

                empty_forward(p, vec, "vec", copy, vec_emptied, between)
                hartley(p, i, lambda t: copy_residual(p, t, i + (B + 2), i * 16 + 16 * (B + 1), 1))
                empty_inverse(p, vec, "vec", copy, vec_emptied)
            mix(2, pass_l1(1))
            with vec.Fori(0, B) as i:
                p = pass_l23(i, 2)
                empty_forward(p, vec, "vec", copy, vec_emptied)
                mlp(p, i, lambda t: copy_residual(p, t, i + (B + 4), i * 16 + 16 * (2 * B + 1), 2))
                empty_inverse(p, vec, "vec", copy, vec_emptied)
                p = pass_l23(i, 3)
                empty_forward(p, vec, "vec", copy, vec_emptied)
                mlp(p, i)
                vec.wait_ge(residual_halved, i + 1)
                empty_inverse(p, vec, "vec", copy, vec_emptied)


def lay_out_conv(w1, b1, w2, b2):
    w3 = np.zeros((P, NB, MROWS), np.float32)
    w4 = np.zeros((MROWS, NB, 2 * BS), np.float32)
    bias = np.zeros((MROWS, NB), np.float32)
    s = slots()
    for b in range(NB):
        for rows, first, second in ((0, 0, 1), (HALF, 1, 0)):
            w3[rows:rows + BS, b, 0:BS] = w1[first, b][s]
            w3[rows:rows + BS, b, HALF:] = w1[second, b][s]
            w4[rows:rows + BS, b, 0:BS] = w2[first, b][:, s]
            w4[rows:rows + BS, b, BS:] = w2[second, b][:, s]
            bias[rows:rows + BS, b] = b1[first, b]
        w4[ONE, b, 0:BS], w4[ONE, b, BS:] = b2[0, b][s], b2[1, b][s]
    bias[ONE] = 1.0
    return w3, w4, bias


def lay_out_hartley(w1, b1, w2, b2):
    first = np.zeros((2, MROWS, NB, MROWS), np.float32)
    first_bias = np.zeros((1, NB, MROWS), np.float32)
    q = np.zeros((2, BS, NB, MROWS), np.float32)
    e = np.zeros((3, BS, NB, BS), np.float32)
    t = np.zeros((2, MROWS, NB, BS), np.float32)
    s = slots()
    for b in range(NB):
        for n in range(2):
            for r in (0, HALF):
                for c in (0, HALF):
                    first[n, r:r + BS, b, c:c + BS] = w1[n, b][s]
                q[n, :, b, r:r + BS] = w2[n, b].T
            e[n, :, b] = w2[n, b][:, s]
            t[n, HALF:, b] = w2[n, b][:, s]
        first_bias[0, b, 0:BS], first_bias[0, b, HALF:] = b1[0, b], b1[1, b]
        first_bias[0, b, ONE] = 1.0
        q[0, :, b, ONE] = b2[0, b]
        t[0, ONE, b] = b2[1, b][s]
        e[2, :, b] = np.eye(BS)[:, s]
    return first, first_bias, q, e, t


def kernel(x, **weights):
    import concourse.bacc as bacc
    from concourse import mybir
    from concourse.bass_utils import run_bass_kernel_spmd

    w = {n: np.asarray(a) for n, a in weights.items()}
    for n in ("L2_conv_w1", "L2_conv_b1", "L2_conv_w2", "L2_conv_b2"):
        w[n] = np.moveaxis(w[n], -1, 0)
    layers = {n: [w[f"L{n}_conv_{k}"] for k in ("w1", "b1", "w2", "b2")] for n in range(4)}
    laid = [lay_out_conv(*layers[n]) for n in (0, 2, 3)]
    first, first_bias, q, e, t = lay_out_hartley(*layers[1])
    parts, fwd_c, inv_c = constants()
    const_at, at = {}, 0
    for name, a in parts.items():
        const_at[name] = (at, a.shape[1])
        at += a.shape[1]
    arrays = {
        "x": np.asarray(x).reshape(B, TOK, P, NT).swapaxes(2, 3).reshape(B, TOK, C),
        "consts": np.concatenate(list(parts.values()), 1),
        "fwd_c": fwd_c,
        "inv_c": inv_c,
        "conv_w3": np.stack([a[0] for a in laid]),
        "conv_w4": np.stack([a[1] for a in laid]),
        "conv_bias": np.stack([a[2] for a in laid]),
        "l1_w3": first.reshape(2, MROWS, -1),
        "l1_w3_bias": first_bias.reshape(1, -1),
        "l1_q": q.reshape(2, BS, -1),
        "l1_e": e.reshape(3, BS, -1),
        "l1_t": t.reshape(2, MROWS, -1),
    }
    arrays = {n: np.ascontiguousarray(a) for n, a in arrays.items()}
    nc = bacc.Bacc("TRN2", target_bir_lowering=False, num_devices=1)
    ins = [nc.dram_tensor(n, a.shape, mybir.dt.float32, kind="ExternalInput").ap() for n, a in arrays.items()]
    out = nc.dram_tensor("out", (B, TOK, C), mybir.dt.float32, kind="ExternalOutput").ap()
    build(nc, *ins, out, const_at)
    r = run_bass_kernel_spmd(nc, [arrays], core_ids=[0])
    return r.results[0]["out"].reshape(B, TOK, NT, P).swapaxes(2, 3).reshape(B, H, W, C)
```
